# Optimizing a Trainium2 kernel written in Bass

```python
import numpy as np
import jax
import jax.numpy as jnp

def _softmax(x, axis=-1):
    return jax.nn.softmax(x, axis=axis)

def _gelu(x):
    return jax.nn.gelu(x, approximate=True)

def _silu(x):
    return jax.nn.silu(x)

def _sigmoid(x):
    return jax.nn.sigmoid(x)

def _layernorm(x, axis=-1, eps=1e-05):
    m = jnp.mean(x, axis=axis, keepdims=True)
    v = jnp.var(x, axis=axis, keepdims=True)
    return (x - m) / jnp.sqrt(v + eps)

def _scatter_add(tgt, idx, src, axis=0):
    return tgt.at[idx].add(src)

def _segment_sum(src, seg, n):
    return jax.ops.segment_sum(src, seg, n)
kernel_name = 'mk_flamingo_gated_d1_seqx_r4_7c1413'

def setup_inputs(seed: int=0):
    np.random.seed(seed)
    _w = jnp.asarray

    def _rec_inputs():
        import jax
        import jax.numpy as jnp
        _rk = jax.random.key(seed)
        x = -0.000125 + 0.9999 * jax.random.normal(jax.random.fold_in(_rk, 1), (4, 512, 512), jnp.float32)
        _lenS = 512 - jax.random.randint(jax.random.fold_in(_rk, 7), (4,), 0, max(1, 512 // 4) + 1, jnp.int32)
        _lenS2 = 512 - jax.random.randint(jax.random.fold_in(_rk, 8), (4,), 0, max(1, 512 // 4) + 1, jnp.int32)
        _ctx_2048P = jax.random.normal(jax.random.fold_in(_rk, 11), (4, 16, 512), jnp.float32)
        _ctx_2048c = jax.random.dirichlet(jax.random.fold_in(_rk, 511), 0.3 * jnp.ones((16,), jnp.float32), (4, 512))
        _ctx_2048t = jnp.einsum('bsk,bkd->bsd', _ctx_2048c, _ctx_2048P)
        _ctx_2048t = _ctx_2048t * jax.lax.rsqrt(jnp.mean(jnp.square(_ctx_2048t)) + 1e-12) * 0.953939
        ctx_2048 = -0.00010331 + 0.999899 * (_ctx_2048t + 0.3 * jax.random.normal(jax.random.fold_in(_rk, 611), (4, 512, 512), jnp.float32))
        _validS = jnp.arange(512)[None, :] < _lenS[:, None]
        _validS2 = jnp.arange(512)[None, :] < _lenS2[:, None]
        _causal = jnp.tril(jnp.ones((512, 512), dtype=bool))
        mask_Bx1xS2_ff0 = jnp.where(jnp.ones((4, 1, 512), dtype=bool), 0.0, -1000000000.0).astype(jnp.float32)
        _g = jax.random.normal(jax.random.fold_in(_rk, 9001), (2, 1), jnp.float32)
        _g = jnp.sign(_g) * jnp.maximum(jnp.abs(_g), 1.0) + (_g == 0) * 1.0
        g_xattn = _g[0]
        g_ffn = _g[1]
        return (x, ctx_2048, mask_Bx1xS2_ff0, g_xattn, g_ffn)
    x, ctx_2048, mask_Bx1xS2_ff0, g_xattn, g_ffn = _rec_inputs()

    def _L0_xattn_setup():
        import jax, jax.numpy as jnp
        import numpy as np
        FP8_E4M3_MAX = 448.0
        EPS = 1e-12

        def _fp8_quant_dequant(x):
            amax = jnp.max(jnp.abs(x))
            scale = FP8_E4M3_MAX / jnp.maximum(amax, EPS)
            q = jnp.clip(x * scale, -FP8_E4M3_MAX, FP8_E4M3_MAX).astype(jnp.float8_e4m3fn)
            return q.astype(jnp.float32) / scale
        key = jax.random.key(seed)
        k1, k2 = jax.random.split(key)
        B, M, K, N = (32, 128, 512, 512)
        inp = jax.random.normal(k1, (B, M, K), dtype=jnp.float32)
        weight = jax.random.normal(k2, (B, K, N), dtype=jnp.float32)
        bias = jnp.zeros((B, 1, N), dtype=jnp.float32)
        return {'input': inp, 'weight': weight, 'bias': bias}
    _L0_xattn_all = _L0_xattn_setup()
    _L0_xattn_in = {k: v for k, v in _L0_xattn_all.items() if k in ()}
    del _L0_xattn_all

    def _L0_ffn_setup():
        import jax, jax.numpy as jnp
        import numpy as np
        B, S, D = (4, 1024, 512)
        E, K, I, J = (8, 2, 352, 1408)
        CAP_FACTOR = 1.25
        STD = 0.02

        def _moe_routed(x_flat, router, w_up_gate, w_down):
            T, d = x_flat.shape
            logits = jnp.einsum('td,de->te', x_flat, router)
            topk_logits, sel = jax.lax.top_k(logits, K)
            cw = jax.nn.softmax(topk_logits, axis=-1).astype(x_flat.dtype)
            C = int(np.ceil(T * K / E * CAP_FACTOR))
            e_flat = sel.reshape(-1)
            oh = jax.nn.one_hot(e_flat, E, dtype=jnp.int32)
            pos_all = jnp.cumsum(oh, axis=0) - oh
            pos = jnp.take_along_axis(pos_all, e_flat[:, None], axis=1)[:, 0]
            valid = pos < C
            safe_pos = jnp.where(valid, pos, C)
            tok = jnp.repeat(jnp.arange(T), K)
            buf = jnp.zeros((E, C, d), x_flat.dtype).at[e_flat, safe_pos].set(x_flat[tok], mode='drop')
            gate_up = jnp.einsum('ecd,edm->ecm', buf, w_up_gate)
            gate, up = jnp.split(gate_up, [I], axis=-1)
            h = jax.nn.silu(gate) * up
            out_buf = jnp.einsum('eci,eid->ecd', h, w_down)
            gathered = out_buf[e_flat, jnp.minimum(safe_pos, C - 1)]
            gathered = gathered * valid[:, None].astype(x_flat.dtype)
            w = cw.reshape(-1)
            y = jnp.zeros((T, d), x_flat.dtype).at[tok].add(w[:, None] * gathered)
            return y

        def _shared_mlp(x_flat, shared_w_up_gate, shared_w_down):
            gu = jnp.einsum('td,dm->tm', x_flat, shared_w_up_gate)
            gate, up = jnp.split(gu, [J], axis=-1)
            return jnp.einsum('tm,md->td', jax.nn.silu(gate) * up, shared_w_down)
        key = jax.random.key(seed)
        kx, kr, ku, kd, ksu, ksd = jax.random.split(key, 6)
        x = jax.random.normal(kx, (B, S, D), dtype=jnp.float32)
        router = STD * jax.random.truncated_normal(kr, -3, 3, (D, E), dtype=jnp.float32)
        w_up_gate = STD * jax.random.truncated_normal(ku, -3, 3, (E, D, 2 * I), dtype=jnp.float32)
        w_down = STD * jax.random.truncated_normal(kd, -3, 3, (E, I, D), dtype=jnp.float32)
        shared_w_up_gate = STD * jax.random.truncated_normal(ksu, -3, 3, (D, 2 * J), dtype=jnp.float32)
        shared_w_down = STD * jax.random.truncated_normal(ksd, -3, 3, (J, D), dtype=jnp.float32)
        return {'x': x, 'router': router, 'w_up_gate': w_up_gate, 'w_down': w_down, 'shared_w_up_gate': shared_w_up_gate, 'shared_w_down': shared_w_down}
    _L0_ffn_all = _L0_ffn_setup()
    _L0_ffn_in = {k: v for k, v in _L0_ffn_all.items() if k in ('router', 'w_up_gate', 'w_down', 'shared_w_up_gate', 'shared_w_down')}
    del _L0_ffn_all
    return {'x': x, 'ctx_2048': ctx_2048, 'mask_Bx1xS2_ff0': mask_Bx1xS2_ff0, 'g_xattn': g_xattn, 'g_ffn': g_ffn, 'L0_ffn_router': _L0_ffn_in['router'], 'L0_ffn_w_up_gate': _L0_ffn_in['w_up_gate'], 'L0_ffn_w_down': _L0_ffn_in['w_down'], 'L0_ffn_shared_w_up_gate': _L0_ffn_in['shared_w_up_gate'], 'L0_ffn_shared_w_down': _L0_ffn_in['shared_w_down']}

def reference(x, ctx_2048, mask_Bx1xS2_ff0, g_xattn, g_ffn, L0_ffn_router, L0_ffn_w_up_gate, L0_ffn_w_down, L0_ffn_shared_w_up_gate, L0_ffn_shared_w_down):
    import jax
    import jax.numpy as jnp

    def _L0_xattn_ref(input, weight, bias):
        import jax, jax.numpy as jnp
        import numpy as np
        FP8_E4M3_MAX = 448.0
        EPS = 1e-12

        def _fp8_quant_dequant(x):
            amax = jnp.max(jnp.abs(x))
            scale = FP8_E4M3_MAX / jnp.maximum(amax, EPS)
            q = jnp.clip(x * scale, -FP8_E4M3_MAX, FP8_E4M3_MAX).astype(jnp.float8_e4m3fn)
            return q.astype(jnp.float32) / scale
        x_dq = _fp8_quant_dequant(input)
        w_dq = _fp8_quant_dequant(weight)
        out = jnp.einsum('bmk,bkn->bmn', x_dq, w_dq)
        out = out + bias
        return out

    def _L0_ffn_ref(x, router, w_up_gate, w_down, shared_w_up_gate, shared_w_down):
        import jax, jax.numpy as jnp
        import numpy as np
        B, S, D = (4, 1024, 512)
        E, K, I, J = (8, 2, 352, 1408)
        CAP_FACTOR = 1.25
        STD = 0.02

        def _moe_routed(x_flat, router, w_up_gate, w_down):
            T, d = x_flat.shape
            logits = jnp.einsum('td,de->te', x_flat, router)
            topk_logits, sel = jax.lax.top_k(logits, K)
            cw = jax.nn.softmax(topk_logits, axis=-1).astype(x_flat.dtype)
            C = int(np.ceil(T * K / E * CAP_FACTOR))
            e_flat = sel.reshape(-1)
            oh = jax.nn.one_hot(e_flat, E, dtype=jnp.int32)
            pos_all = jnp.cumsum(oh, axis=0) - oh
            pos = jnp.take_along_axis(pos_all, e_flat[:, None], axis=1)[:, 0]
            valid = pos < C
            safe_pos = jnp.where(valid, pos, C)
            tok = jnp.repeat(jnp.arange(T), K)
            buf = jnp.zeros((E, C, d), x_flat.dtype).at[e_flat, safe_pos].set(x_flat[tok], mode='drop')
            gate_up = jnp.einsum('ecd,edm->ecm', buf, w_up_gate)
            gate, up = jnp.split(gate_up, [I], axis=-1)
            h = jax.nn.silu(gate) * up
            out_buf = jnp.einsum('eci,eid->ecd', h, w_down)
            gathered = out_buf[e_flat, jnp.minimum(safe_pos, C - 1)]
            gathered = gathered * valid[:, None].astype(x_flat.dtype)
            w = cw.reshape(-1)
            y = jnp.zeros((T, d), x_flat.dtype).at[tok].add(w[:, None] * gathered)
            return y

        def _shared_mlp(x_flat, shared_w_up_gate, shared_w_down):
            gu = jnp.einsum('td,dm->tm', x_flat, shared_w_up_gate)
            gate, up = jnp.split(gu, [J], axis=-1)
            return jnp.einsum('tm,md->td', jax.nn.silu(gate) * up, shared_w_down)
        b, s, d = x.shape
        x_flat = x.reshape(b * s, d)
        routed = _moe_routed(x_flat, router, w_up_gate, w_down)
        shared = _shared_mlp(x_flat, shared_w_up_gate, shared_w_down)
        return (routed + shared).reshape(b, s, d)
    x = x + jnp.tanh(g_xattn[0]) * _L0_xattn_ref(_layernorm(x, axis=-1), ctx_2048, mask_Bx1xS2_ff0)
    x = x + jnp.tanh(g_ffn[0]) * _L0_ffn_ref(_layernorm(x, axis=-1), L0_ffn_router, L0_ffn_w_up_gate, L0_ffn_w_down, L0_ffn_shared_w_up_gate, L0_ffn_shared_w_down)
    return x

_drawn_inputs = setup_inputs


def setup_inputs(seed=0):
    import zlib

    import numpy as np

    out = dict(_drawn_inputs(seed))
    spreads = {}
    factors = {'L0_ffn_router': 8.0,
     'L0_ffn_w_up_gate': 8.0,
     'L0_ffn_w_down': 8.0,
     'L0_ffn_shared_w_up_gate': 8.0,
     'L0_ffn_shared_w_down': 8.0}
    for name, (base, spread) in spreads.items():
        noise = np.random.default_rng([zlib.crc32(name.encode()), seed]).standard_normal(out[name].shape)
        drawn = base * np.exp(spread * noise) if base else spread * noise
        out[name] = jnp.asarray(drawn.astype(out[name].dtype))
    for name, factor in factors.items():
        out[name] = (out[name] * factor).astype(out[name].dtype)
    return out
```

```python
from contextlib import ExitStack

import concourse.bass as bass
from concourse import mybir

ALU = mybir.AluOpType
ACT = mybir.ActivationFunctionType
AX = mybir.AxisListType
F32 = mybir.dt.float32
F16 = mybir.dt.float16
BF16 = mybir.dt.bfloat16
U32 = mybir.dt.uint32

P = 128
EPS_LN = 1e-5
EPS_Q = 1e-12
FP8_MAX = 448.0
H_SCALE = 2.0 ** 8
W_SCALE = 2.0 ** 6
ROUND_UP = 2.0 ** 20
ROUND_FLOOR = 1.5 * 2.0 ** 14
EXP_MASK = 0x7F800000
HALF_BIT = 0x00400000
PARTS = ((0, 0), (0, 1), (1, 0))
FAR = 1.0e6


def build_flamingo(nc, x, ctx_in, mask, g_x, g_f, router, w_ug, w_dn, sw_ug, sw_dn, out):
    B, S, D = x.shape
    E, _, I2 = w_ug.shape
    I = I2 // 2
    J = sw_dn.shape[0]
    T = B * S
    NT = T // P
    TB = S // P
    KD = D // P
    MS = J // P
    ME = -(-I // P)
    EC = [min(P, I - c * P) for c in range(ME)]
    TOPK = 2
    CAP = -(-T * TOPK * 5 // (E * 4))
    CT = CAP // P
    HC = CAP // 2
    UNIT = KD * 2 * P + D
    UW = KD * 2 * P
    FIRST_CHUNK_STEP = TB + 2
    assert T == 2048 and D == 512 and CT * P == CAP and MS == 11 and ME == 3 and TB == 4

    x1_dram = nc.dram_tensor("x1_scratch", (T, D), F32, kind="Internal").ap()
    h_dram = nc.dram_tensor("h_scratch", (T, D), F32, kind="Internal").ap()
    slot_dram = nc.dram_tensor("slot_scratch", (E * CAP, 1), U32, kind="Internal").ap()
    eo_dram = nc.dram_tensor("expert_out_scratch", (E * CAP, D), F32, kind="Internal").ap()

    es = ExitStack()
    with es:
        def sb(name, shape, dt):
            return es.enter_context(nc.sbuf_tensor(name, shape, dt))

        def sem(name):
            return es.enter_context(nc.semaphore(name))

        tok = sb("tok", [P, NT, D], F32)
        h_split = tok[:].rearrange("p t d -> p (t d)").bitcast(F16).rearrange(
            "p (t s k n) -> p t s k n", t=NT, s=2, k=KD)
        xe = tok[:, 0:CT, :].rearrange("p t d -> p (t d)").bitcast(F16).rearrange(
            "p (s k n) -> p s k n", s=2, k=KD)
        sw = sb("sw", [P, MS, 2, KD, 2, P], F16)
        sd = sb("sd", [P, MS, 2, D], F16)
        act_reg = sb("act_reg", [P, MS * 2 * D], F16)
        a_sh = act_reg[:].rearrange("p (m s n) -> p m s n", m=MS, s=2)
        a_ex = act_reg[:, 0:ME * 2 * CAP].rearrange("p (m s n) -> p m s n", m=ME, s=2)
        o_ex = act_reg[:, ME * 2 * CAP:ME * 2 * CAP + CT * D * 2].bitcast(F32).rearrange(
            "p (j d) -> p j d", j=CT)
        n_ew = 2 * ME * 2 * KD * 2 * P
        n_ed = 2 * ME * 2 * D
        ewr = sb("expert_w", [P, n_ew + n_ed], F16)
        ew = ewr[:, 0:n_ew].rearrange("p (b m s k g n) -> p b m s k g n", b=2, m=ME, s=2, k=KD, g=2)
        ed = ewr[:, n_ew:n_ew + n_ed].rearrange("p (b m s n) -> p b m s n", b=2, m=ME, s=2)
        ctx_raw = ewr[:, 0:B * KD * D * 2].bitcast(F32).rearrange("p (c n) -> p c n", c=B * KD)
        ctx_q = ewr[:, 0:B * KD * D * 2].bitcast(BF16).rearrange("p (c n) -> p c n", c=B * KD)
        pv = sw[:, MS - 2:MS].rearrange("p m s k g n -> p (m s k g n)").bitcast(F32).rearrange("p (b s n) -> p b s n", b=2, s=2)
        grow = sb("gathered", [P, CT, D], F32)
        v20 = grow[:, 0:2, :]
        h_tok = grow[:, 2:4, :]
        q_tok = grow[:, 4, :].bitcast(BF16).rearrange("p (b d) -> p b d", b=2)
        comb = grow[:, 0:4, :].rearrange("p (b k) d -> p b k d", b=2)
        base = sb("base", [P, 4 + 2 * UNIT // D, D], F32)
        raw = base[:, 4:4 + 2 * UNIT // D, :].rearrange("p a d -> p (a d)").rearrange(
            "p (b u) -> p b u", b=2)
        sg = sb("silu_gate", [P, 2, D], F32)
        mask_row = sg[0:B, 0, :]
        mask_res = base[0:B, 0:3, :]
        qT = sb("qT", [P, 2, KD, P], BF16)
        id_f = sb("ident_f32", [P, P], F32)
        id_b = sb("ident_bf16", [P, P], BF16)
        before = sb("before", [P, P], BF16)
        ones_b = sb("ones_bf16", [P, P], BF16)
        mask_b = sb("mask_parts", [B, 3, D], BF16)
        mask_p = sb("mask_stack", [3 * B, D], BF16)
        pick = sb("pick_batch", [3 * B, B, P], BF16)
        r_raw = sb("router_raw", [P, KD, E], F32)
        r_split = sb("router_split", [P, KD, 2 * E], F16)
        tg = sb("tanh_gates", [P, 2], F32)
        tg_raw = sb("gates_raw", [P, 2], F32)
        tgw = sb("ffn_gate_scaled", [P, 1], F32)
        carry_a = sb("carry_a", [P, 2], F32)
        carry_v = sb("carry_v", [P, 1], F32)
        carry_p = sb("carry_p", [P, 3], F32)
        st1 = sb("stats1", [P, NT, 6], F32)
        mv1 = sb("meanvar1", [P, NT, 2], F32)
        ln1 = sb("rstd_shift1", [P, 4, NT], F32)
        nhalf = sb("minus_half", [P, NT], F32)
        zmax = sb("zmax", [P, NT + B], F32)
        amax = sb("amax", [P, 2], F32)
        gmax = sb("gmax", [P, 2], F32)
        sc = sb("scales", [P, 8], F32)
        vsc = sb("quant_scale", [P, 2, NT], F32)
        st2 = sb("stats2", [P, 2, 6], F32)
        mv2 = sb("meanvar2", [P, 2, 2], F32)
        ln2 = sb("rstd_shift2", [P, 2, 4], F32)
        lg = sb("logits", [P, NT, E], F32)
        top_v = sb("top_values", [P, NT, E], F32)
        top_i = sb("top_index", [P, NT, E], U32)
        sel = sb("expert_of", [P, NT, TOPK], F32)
        hot = sb("one_hot", [P, NT, TOPK, E], F32)
        hot_n = sb("count_rows", [P, NT, E], BF16)
        seat = sb("seat_products", [P, NT, TOPK, E], F32)
        pos = sb("position", [P, NT * TOPK], F32)
        valid = sb("valid", [P, NT * TOPK], F32)
        slot_f = sb("slot_f", [P, NT * TOPK], F32)
        to_slot = sb("scatter_slot", [P, NT * TOPK], U32)
        from_slot = sb("gather_slot", [P, NT * TOPK], U32)
        dlt = sb("logit_gap", [P, NT], F32)
        ex2 = sb("exp_gap", [P, NT], F32)
        wsum = sb("weight_sum", [P, NT], F32)
        cw = sb("combine_w", [P, NT, TOPK], F32)
        iota_e = sb("iota_e", [P, E], F32)
        tok_id = sb("token_id", [P, NT], U32)
        zero_i = sb("zero_slots", [P, E * CT], U32)
        slot_tok = sb("slot_token", [P, E, CT], U32)

        gu = es.enter_context(nc.psum_tensor("gu", [P, 2, 2, D], F32))
        gu4 = gu[:].rearrange("p a g n -> p (a g) n")
        dn = es.enter_context(nc.psum_tensor("dn", [P, 2, D], F32))
        tp = es.enter_context(nc.psum_tensor("tp", [P, 2, D], F32))
        tp_q = tp[:, 0, 0:D // 2].bitcast(BF16).rearrange("p (k n) -> p k n", k=KD)
        tp_h = tp[:, 1, :].rearrange("p (k n) -> p k n", k=KD)
        tp_r = tp[:, 0, D // 2:D].rearrange("p (t c) -> p t c", t=NT)
        tp_x = tp[:].rearrange("p b (k n) -> p b k n", k=KD)
        tp_pos = tp[:, 1, 0:NT * E]

        x_in = [sem(f"x_in{b}") for b in range(B)]
        x_first = [sem(f"x_first{t}") for t in range(TB)]
        c_in = [sem(f"c_in{b}") for b in range(B)]
        small_in = sem("small_in")
        consts = sem("consts")
        zero_done = sem("zero_done")
        table_zeroed = sem("table_zeroed")
        gates_done = sem("gates_done")
        tgw_done = sem("tgw_done")
        router_hi = sem("router_hi")
        router_done = sem("router_done")
        mask_done = sem("mask_done")
        mask_in = sem("mask_in")
        bn1 = sem("bn1")
        mv1_done = sem("mv1_done")
        ln1_done = sem("ln1_done")
        absz_done = sem("absz_done")
        zmax_done = sem("zmax_done")
        cmax_done = sem("cmax_done")
        pv_done = sem("pool_v_done")
        pbits_done = sem("pool_bits_done")
        pround = sem("pool_round_steps")
        pq_done = sem("pool_q_done")
        amax_done = sem("amax_done")
        gmax_done = sem("gmax_done")
        scale_done = sem("scale_done")
        v_done = sem("v_done")
        v20_done = sem("v20_done")
        bits_done = sem("bits_done")
        sum_done = sem("sum_done")
        q_done = sem("q_done")
        qT_ps = sem("qT_in_psum")
        qT_done = sem("qT_done")
        xa_ps = sem("attn_in_psum")
        x1_done = sem("x1_done")
        bn2 = sem("bn2")
        mv2_done = sem("mv2_done")
        ln2_done = sem("ln2_done")
        h_done = sem("h_done")
        x1_stored = [sem(f"x1_stored{i}") for i in range(2)]
        h_stored = [sem(f"h_stored{i}") for i in range(2)]
        hT_ps = sem("hT_in_psum")
        hhi_done = sem("h_hi_done")
        hlo_done = sem("h_lo_done")
        rt_ps = sem("logits_in_psum")
        raw_in = [sem(f"raw_in{i}") for i in range(2)]
        whi_done = sem("w_hi_done")
        wsc_done = sem("w_scaled")
        wlo_done = sem("w_lo_done")
        gu_ps = sem("gate_up_in_psum")
        silu_done = sem("silu_done")
        prod_done = sem("product_done")
        ahi_done = sem("act_hi_done")
        alo_done = sem("act_lo_done")
        dn_ps = sem("down_in_psum")
        base_in = [sem(f"base_in{i}") for i in range(TB)]
        y_done = sem("y_done")
        y_stored = [sem(f"y_stored{i}") for i in range(2)]
        rstep = sem("routing_steps")
        cnt_ready = sem("counts_ready")
        pos_ps = sem("positions_in_psum")
        gap_done = sem("gap_done")
        exp_done = sem("exp_done")
        slots_done = sem("slots_done")
        weights_done = sem("combine_weights_done")
        scattered = sem("scattered")
        table_in = sem("table_in")
        g_in = sem("gathered_in")
        xT_ps = sem("xT_in_psum")
        xhi_done = sem("x_hi_done")
        xlo_done = sem("x_lo_done")
        o_ps = sem("expert_out_in_psum")
        o_done = sem("expert_out_done")
        o_stored = sem("expert_out_stored")
        cbase_in = sem("comb_base_in")
        cring_in = [sem(f"comb_ring_in{i}") for i in range(2)]
        cg_in = [sem(f"comb_rows_in{i}") for i in range(2)]
        c1_done = sem("comb_first_done")
        c_done = sem("comb_done")
        out_stored = [sem(f"out_stored{i}") for i in range(2)]

        NQC = B * KD
        LAST_CTX_STEP = NQC - 5
        PS = FIRST_CHUNK_STEP

        def seq_ctx(i):
            return 4 + PS + 2 * (i - PS)

        def seq_x(i):
            if isinstance(i, int) and i < PS:
                return 4 + i
            return seq_ctx(i) - 1 if not isinstance(i, int) or i <= LAST_CTX_STEP else \
                seq_ctx(LAST_CTX_STEP) + i - LAST_CTX_STEP

        def x_ready(t):
            if not isinstance(t, int):
                return seq_x(t - 1) + 1
            return 3 + t if t < 2 else seq_x(t - 2) + 1 if t < PS + 2 else seq_x(t - 1) + 1

        JOB_E = 2 * MS
        JOB_2 = JOB_E + 2 * ME * E

        def block_job(b):
            return b * MS if b < 2 else JOB_2 + (b - 2) * MS

        NU = MS + E * ME

        x_v = x.rearrange("b (j p) d -> b p j d", p=P)
        c_v = ctx_in.rearrange("b (k p) n -> b p k n", p=P)
        x1_v = x1_dram.rearrange("(t p) d -> p t d", p=P)
        h_v = h_dram.rearrange("(t p) d -> p t d", p=P)
        out_v = out.rearrange("b (j p) d -> p (b j) d", p=P)
        swv = sw_ug.rearrange("(k p) (g m n) -> p m k g n", p=P, g=2, n=P)
        sdv = sw_dn.rearrange("(m p) d -> p m d", p=P)
        ewv = w_ug.rearrange("e (k p) (g n) -> p e k g n", p=P, g=2)
        table_v = slot_dram.rearrange("(e p j) o -> p e (j o)", p=P, j=CT)
        eo_v = eo_dram.rearrange("(e p j) d -> p e (j d)", p=P, j=CT)

        block = es.enter_context(nc.Block())

        def raw_w(slot, cols):
            return raw[:, slot, 0:UW].rearrange("p (k g n) -> p k g n", k=KD, g=2)[:, :, :, 0:cols]

        def raw_d(slot, rows):
            return raw[0:rows, slot, UW:UNIT]

        def stages(i):
            if not isinstance(i, int):
                return dict(q=True, ctx=True, tq=True, xa=True, th=True, rt=True)
            return dict(q=i < PS or PS < i < NT - 1, ctx=i <= LAST_CTX_STEP, tq=i < NT, xa=1 <= i <= NT,
                        th=2 <= i <= NT + 1, rt=3 <= i <= NT + 2)

        def v_bank(seq, alone):
            return (gu4[:, seq % 4, :], 4) if alone else (dn[:, 1, :], 1)

        @block.sync
        def _(sp):
            def load_unit_shared(m, slot, half, first=False):
                if not first:
                    sp.wait_ge(wlo_done, 2 * (2 * half + slot - 1))
                sp.dma_start(raw[:, slot, 0:UW].rearrange("p (k g n) -> p k g n", k=KD, g=2)[:, :, 0, :],
                             swv[:, m, :, 0, :]).then_inc(raw_in[slot], 16)
                sp.dma_start(raw[:, slot, 0:UW].rearrange("p (k g n) -> p k g n", k=KD, g=2)[:, :, 1, :],
                             swv[:, m, :, 1, :]).then_inc(raw_in[slot], 16)
                sp.dma_start(raw_d(slot, P), sdv[:, m, :]).then_inc(raw_in[slot], 16)

            def load_unit_expert(e, c, slot, half):
                sp.wait_ge(wlo_done, 2 * (2 * half + slot - 1))
                n = EC[c]
                for g in range(2):
                    sp.dma_start(raw_w(slot, n)[:, :, g, :],
                                 ewv[:, e, :, g, c * P:c * P + n]).then_inc(raw_in[slot], 16)
                sp.dma_start(raw_d(slot, n), w_dn[e, c * P:c * P + n, :]).then_inc(raw_in[slot], 16)

            def store_tile(t, par):
                sp.wait_ge(x1_done, t + 1)
                sp.dma_start(x1_v[:, t, :], tok[:, t, :]).then_inc(x1_stored[par], 16)
                sp.wait_ge(h_done, t + 1)
                sp.dma_start(h_v[:, t, :], h_tok[:, par, :]).then_inc(h_stored[par], 16)

            sp.dma_start(tg_raw[:, 0:1], g_x.rearrange("(a o) -> a o", o=1).to_broadcast([P, 1])).then_inc(small_in, 16)
            sp.dma_start(tg_raw[:, 1:2], g_f.rearrange("(a o) -> a o", o=1).to_broadcast([P, 1])).then_inc(small_in, 16)
            sp.dma_start(mask_row, mask.rearrange("b o d -> (b o) d")).then_inc(small_in, 16)
            sp.dma_start(r_raw[:], router.rearrange("(k p) e -> p k e", p=P)).then_inc(small_in, 16)
            for t in range(TB):
                sp.dma_start(tok[:, t, :], x_v[0][:, t, :]).then_inc(x_first[t], 16)
            for b in range(1, B):
                sp.dma_start(tok[:, b * TB:(b + 1) * TB, :], x_v[b]).then_inc(x_in[b], 16)
            for b in range(B):
                sp.dma_start(ctx_raw[:, b * KD:(b + 1) * KD, :], c_v[b]).then_inc(c_in[b], 16)
            load_unit_shared(0, 0, 0, first=True)
            load_unit_shared(1, 1, 0, first=True)
            sp.wait_ge(zero_done, 1)
            sp.dma_start(table_v, zero_i[:].rearrange("p (e j) -> p e j", e=E)).then_inc(table_zeroed, 16)

            sp.wait_ge(mask_done, 6)
            for a in range(3):
                sp.dma_start(mask_p[a * B:(a + 1) * B, :], mask_b[:, a, :]).then_inc(mask_in, 16)

            for i in range(1, 6):
                store_tile(i - 1, (i - 1) % 2)
                if i == 5:
                    load_unit_shared(2, 0, 1)
            load_unit_shared(3, 1, 1)
            with sp.Fori(0, 3) as r:
                for h in range(2):
                    store_tile(5 + 2 * r + h, (5 + h) % 2)
                    load_unit_shared(4 + 2 * r + h, h, r + 2)
            for i in range(12, 17):
                store_tile(i - 1, (i - 1) % 2)
                if i == 12:
                    load_unit_shared(10, 0, 5)

            def load_expert_unit_after(u):
                e, c = divmod(u - MS, ME)
                load_unit_expert(e, c, u % 2, u // 2)

            def load_base(b, j):
                y = b * TB + j
                if b:
                    sp.wait_ge(y_stored[j % 2], 16 * (2 * b))
                sp.dma_start(base[:, j, :], x1_v[:, y, :]).then_inc(base_in[j], 16)

            def store_y(b, j):
                sp.wait_ge(y_done, b * TB + j + 1)
                sp.dma_start(x1_v[:, b * TB + j, :], base[:, j, :]).then_inc(y_stored[j % 2], 16)

            for u in (MS, MS + 1):
                load_expert_unit_after(u)
            for par in range(2):
                sp.wait_ge(x1_stored[par], 16 * NT // 2)
                sp.wait_ge(h_stored[par], 16 * NT // 2)
            for j in range(TB):
                load_base(0, j)
            for j in range(TB):
                store_y(0, j)
            for j in range(TB):
                load_base(1, j)
            sp.wait_ge(scattered, 16 * NT * TOPK)
            sp.dma_start(slot_tok[:], table_v).then_inc(table_in, 16)
            load_expert_unit_after(MS + 2)
            load_expert_unit_after(MS + 3)
            for j in range(TB):
                store_y(1, j)
            load_expert_unit_after(MS + 4)

            def store_expert(e):
                sp.wait_ge(o_done, CT * (e + 1))
                sp.dma_start(eo_v[:, e, :], o_ex.rearrange("p j d -> p (j d)")).then_inc(o_stored, 16)

            def expert_step(e, h, r, last=False):
                for c in range(ME):
                    k = MS + ME * (h + 1) + c + 2
                    if isinstance(r, int) and k + 2 * ME * r >= NU:
                        continue
                    cc = (c + 2) % ME
                    load_unit_expert(e + 1 + (c + 2) // ME, cc, k % 2, r * ME + k // 2)
                store_expert(e)

            for par in range(2):
                sp.wait_ge(y_stored[par], 16 * TB)
            for q in range(TB):
                sp.dma_start(base[:, q, :], x1_v[:, 8 + q, :]).then_inc(cbase_in, 16)
            with sp.Fori(0, E // 2 - 1) as r:
                for h in range(2):
                    expert_step(2 * r + h, h, r)
            for h in range(2):
                expert_step(E - 2 + h, h, E // 2 - 1)

            sp.wait_ge(wlo_done, 2 * NU)
            for q in range(TB, 8):
                sp.dma_start(base[:, q, :], x1_v[:, 8 + q, :]).then_inc(cbase_in, 16)
            for q in range(8, 16):
                if q >= 10:
                    sp.wait_ge(c_done, q - 1)
                    sp.dma_start(out_v[:, q - 10, :], base[:, q % 2 + 8, :]).then_inc(out_stored[q % 2], 16)
                    sp.wait_ge(out_stored[q % 2], 16 * ((q - 8) // 2))
                sp.dma_start(base[:, q % 2 + 8, :], x1_v[:, q - 8, :]).then_inc(cring_in[q % 2], 16)
            for q in range(14, 16):
                sp.wait_ge(c_done, q + 1)
                sp.dma_start(out_v[:, q - 8, :], base[:, q % 2 + 8, :]).then_inc(out_stored[q % 2], 16)
            for j in range(2 * TB):
                sp.wait_ge(y_done, 2 * TB + j + 1)
                sp.dma_start(out_v[:, 2 * TB + j, :], base[:, j, :]).then_inc(out_stored[j % 2], 16)
            for par in range(2):
                sp.wait_ge(out_stored[par], 16 * NT // 2)

        @block.gpsimd
        def _(pool):
            pool.memset(zero_i[:], 0).then_inc(zero_done, 1)
            pool.memset(id_f[:], 0.0).then_inc(consts, 1)
            pool.memset(ones_b[:], 1.0).then_inc(consts, 1)
            pool.memset(nhalf[:], -0.5).then_inc(consts, 1)
            pool.memset(pick[:], 0.0).then_inc(consts, 1)
            pool.iota(tok_id[:], pattern=[[P, NT]], base=0, channel_multiplier=1).then_inc(consts, 1)
            pool.iota(iota_e[:], pattern=[[1, E]], base=0, channel_multiplier=0,
                      allow_small_or_imprecise_dtypes=True).then_inc(consts, 1)
            pool.wait_ge(consts, 6)
            pool.affine_select(out=id_f[:], in_=id_f[:], pattern=[[-1, P]], compare_op=ALU.not_equal,
                               fill=1.0, base=0, channel_multiplier=1).then_inc(consts, 1)
            pool.affine_select(out=before[:], in_=ones_b[:], pattern=[[1, P]], compare_op=ALU.is_gt,
                               fill=0.0, base=0, channel_multiplier=-1).then_inc(consts, 1)
            for a in range(3):
                pool.affine_select(out=pick[:], in_=pick[:], pattern=[[-1, B], [0, P]], compare_op=ALU.not_equal,
                                   fill=1.0, base=-a * B, channel_multiplier=1).then_inc(consts, 1)
                pool.wait_ge(consts, 9 + a)
            pool.tensor_copy(id_b[:], id_f[:]).then_inc(consts, 1)

            def held(col=0):
                pool.tensor_tensor(carry_p[:, col:col + 1], nhalf[:, 0:1], nhalf[:, 1:2], ALU.add)

            def rstd_shift(mean, var, tmp, rstd, neg, shift, n, s, k0):
                held()
                pool.tensor_scalar(tmp, var, EPS_LN, 1.0, ALU.add, ALU.mult).then_inc(s, 1)
                pool.tensor_scalar(neg, mean, -1.0, 1.0, ALU.mult, ALU.mult).then_inc(s, 1)
                pool.wait_ge(s, k0 + 2)
                pool.tensor_tensor(rstd, tmp, nhalf[:, 0:n], ALU.pow).then_inc(s, 1)
                pool.wait_ge(s, k0 + 3)
                pool.tensor_tensor(shift, neg, rstd, ALU.mult).then_inc(s, 1)

            for b in range(B):
                t = slice(b * TB, (b + 1) * TB)
                pool.wait_ge(mv1_done, (b + 1) * TB)
                rstd_shift(mv1[:, t, 0], mv1[:, t, 1], ln1[:, 2, t], ln1[:, 0, t], ln1[:, 3, t],
                           ln1[:, 1, t], TB, ln1_done, 4 * b)
            def w_scale(u, slot, n):
                pool.wait_ge(whi_done, 2 * u + 2)
                held(1 + slot)
                rw, rd = raw_w(slot, n), raw_d(slot, n)
                pool.tensor_scalar(rw, rw, W_SCALE, 1.0, ALU.mult, ALU.mult).then_inc(wsc_done, 1)
                pool.tensor_scalar(rd, rd, W_SCALE, 1.0, ALU.mult, ALU.mult).then_inc(wsc_done, 1)

            def low_w(u, slot, dst_w, n):
                pool.wait_ge(wsc_done, 2 * u + 1)
                pool.tensor_tensor(dst_w[:, 1, :, :, 0:n], raw_w(slot, n), dst_w[:, 0, :, :, 0:n],
                                   ALU.subtract).then_inc(wlo_done, 1)

            def low_d(u, slot, dst_d, n):
                pool.wait_ge(wsc_done, 2 * u + 2)
                pool.tensor_tensor(dst_d[0:n, 1, :], raw_d(slot, n), dst_d[0:n, 0, :],
                                   ALU.subtract).then_inc(wlo_done, 1)

            def w_low(u, slot, dst_w, dst_d, n):
                w_scale(u, slot, n)
                low_w(u, slot, dst_w, n)
                low_d(u, slot, dst_d, n)

            def w_low_shared(m, slot):
                w_low(m, slot, sw[:, m], sd[:, m], P)

            w_scale(0, 0, P)
            pool.wait_ge(amax_done, 2)
            pool.partition_all_reduce(gmax[:], amax[:], P, bass.bass_isa.ReduceOp.max).then_inc(gmax_done, 1)
            w_scale(1, 1, P)

            pool.wait_ge(small_in, 64)
            pool.wait_ge(gmax_done, 5)
            held()
            pool.tensor_scalar(mask_res[:, 0, :], mask_row, sc[0:B, 2:3], 1.0, ALU.mult, ALU.mult).then_inc(
                mask_done, 1)
            for i in range(3):
                pool.wait_ge(mask_done, 1 + 2 * i)
                pool.tensor_scalar(mask_b[:, i, :], mask_res[:, i, :], 1.0, 1.0, ALU.mult, ALU.mult).then_inc(
                    mask_done, 1)
                if i < 2:
                    pool.wait_ge(mask_done, 2 + 2 * i)
                    pool.tensor_tensor(mask_res[:, i + 1, :], mask_res[:, i, :], mask_b[:, i, :],
                                       ALU.subtract).then_inc(mask_done, 1)

            def round_ctx(c, seq):
                v, v20p = pv[:, seq % 2, 0, :], pv[:, seq % 2, 1, :]
                pool.wait_ge(pbits_done, 2 * seq + 2)
                pool.tensor_tensor(v, v20p, v, ALU.add).then_inc(pround, 1)
                pool.wait_ge(pround, seq + 1)
                pool.tensor_tensor(ctx_q[:, c, 0:D], v20p, v, ALU.subtract).then_inc(pq_done, 1)

            round_ctx(1, 0)
            round_ctx(3, 1)
            round_ctx(4, 2)

            def ln_small(t, par):
                pool.wait_ge(mv2_done, t + 1)
                if not isinstance(t, int) or t >= 2:
                    pool.wait_ge(h_done, t - 1)
                rstd_shift(mv2[:, par, 0:1], mv2[:, par, 1:2], ln2[:, par, 2:3], ln2[:, par, 0:1],
                           ln2[:, par, 3:4], ln2[:, par, 1:2], 1, ln2_done, 4 * t)

            def w_low_expert(u, slot, par, c):
                w_low(u, slot, ew[:, par, c], ed[:, par, c], EC[c])

            low_w(0, 0, sw[:, 0], P)
            for i in range(1, PS):
                ln_small(i - 1, (i - 1) % 2)
                round_ctx(i + 4, i + 2)
                if i == 1:
                    low_d(0, 0, sd[:, 0], P)
                if i == 2:
                    low_w(1, 1, sw[:, 1], P)
                if i == 3:
                    low_d(1, 1, sd[:, 1], P)
            with pool.Fori(0, 4) as r:
                for h in range(2):
                    ln_small(5 + 2 * r + h, (5 + h) % 2)
                    w_low_shared(2 + 2 * r + h, h)
            ln_small(13, 1)
            w_low_shared(MS - 1, 0)
            ln_small(14, 0)
            ln_small(15, 1)

            pool.wait_ge(table_zeroed, 16)
            pool.wait_ge(slots_done, 2)
            for t in range(NT):
                for k in range(TOPK):
                    i = TOPK * t + k
                    pool.indirect_dma_start(
                        out=slot_dram, out_offset=bass.IndirectOffsetOnAxis(ap=to_slot[:, i:i + 1], axis=0),
                        in_=tok_id[:, t:t + 1], in_offset=None, bounds_check=E * CAP - 1,
                        oob_is_err=False).then_inc(scattered, 16)
            for c in range(2):
                w_low_expert(MS + c, (MS + c) % 2, 0, c)

            def gather_expert(e):
                if e:
                    pool.wait_ge(xT_ps, CT * e)
                for j in range(CT):
                    pool.indirect_dma_start(
                        out=grow[:, j, :], out_offset=None, in_=h_dram,
                        in_offset=bass.IndirectOffsetOnAxis(ap=slot_tok[:, e, j:j + 1], axis=0),
                        bounds_check=T - 1, oob_is_err=False).then_inc(g_in, 16)

            pool.wait_ge(table_in, 16)
            gather_expert(0)
            w_low_expert(MS + 2, (MS + 2) % 2, 0, 2)
            for e in range(E):
                if e + 1 < E:
                    gather_expert(e + 1)
                    for c in range(ME):
                        u = MS + ME * (e + 1) + c
                        w_low_expert(u, u % 2, (e + 1) % 2, c)

            pool.wait_ge(o_stored, 16 * E)
            pool.wait_ge(xT_ps, CT * E)
            for q in range(NT):
                t = (q + NT // 2) % NT
                if q >= 2:
                    pool.wait_ge(c_done, q - 1)
                for k in range(TOPK):
                    i = TOPK * t + k
                    pool.indirect_dma_start(
                        out=comb[:, q % 2, k, :], out_offset=None, in_=eo_dram,
                        in_offset=bass.IndirectOffsetOnAxis(ap=from_slot[:, i:i + 1], axis=0),
                        bounds_check=E * CAP - 1, oob_is_err=False).then_inc(cg_in[q % 2], 16)

        @block.scalar
        def _(act):
            act.wait_ge(small_in, 64)
            act.activation(carry_a[:], tg_raw[:], ACT.Silu)
            act.activation(tg[:], tg_raw[:], ACT.Tanh).then_inc(gates_done, 1)
            act.mul(r_split[:, :, 0:E], r_raw[:], W_SCALE).then_inc(router_hi, 1)
            for t in range(NT):
                act.wait_ge(ln1_done, 4 * (t // TB + 1))
                if t >= 4:
                    act.wait_ge(zmax_done, t - 3)
                act.activation(gu4[:, t % 4, :], tok[:, t, :], ACT.Abs, bias=ln1[:, 1, t:t + 1],
                               scale=ln1[:, 0, t:t + 1]).then_inc(absz_done, 1)

            def quant(seq, par, alone, src, scale, bias):
                bank, depth = v_bank(seq, alone)
                if not isinstance(seq, int) or seq >= depth:
                    act.wait_ge(q_done, seq + 1 - depth)
                act.activation(bank, src, ACT.Identity, bias=bias, scale=scale).then_inc(v_done, 1)
                act.wait_ge(v_done, seq + 1)
                if depth > 1 and seq >= 2:
                    act.wait_ge(q_done, seq - 1)
                act.activation(v20[:, par, :], bank, ACT.Copy, scale=ROUND_UP).then_inc(v20_done, 1)

            def quant_ctx(c, seq, par, alone):
                quant(seq, par, alone, ctx_raw[:, c, :], sc[:, 1:2], 0.0)

            def quant_ctx_pool(c, seq):
                if seq >= 2:
                    act.wait_ge(pq_done, seq - 1)
                act.activation(pv[:, seq % 2, 0, :], ctx_raw[:, c, :], ACT.Identity, bias=0.0,
                               scale=sc[:, 1:2]).then_inc(pv_done, 1)
                act.wait_ge(pv_done, 2 * seq + 1)
                act.activation(pv[:, seq % 2, 1, :], pv[:, seq % 2, 0, :], ACT.Copy,
                               scale=ROUND_UP).then_inc(pv_done, 1)

            def quant_x(t, seq, par, alone):
                quant(seq, par, alone, tok[:, t, :], vsc[:, 0, t:t + 1] if isinstance(t, int) else
                      vsc[:, 0, bass.ds(t, 1)], vsc[:, 1, t:t + 1] if isinstance(t, int) else
                      vsc[:, 1, bass.ds(t, 1)])

            def w_high(u, slot, half, dst_w, dst_d, n):
                act.wait_ge(raw_in[slot], 48 * (half + 1))
                act.mul(dst_w[:, 0, :, :, 0:n], raw_w(slot, n), W_SCALE).then_inc(whi_done, 1)
                act.mul(dst_d[0:n, 0, :], raw_d(slot, n), W_SCALE).then_inc(whi_done, 1)

            def silu(n, par, dst, rows, cols):
                act.wait_ge(gu_ps, n + 1)
                act.activation(sg[0:rows, par, 0:cols], gu[0:rows, par, 0, 0:cols], ACT.Silu,
                               scale=1.0 / (H_SCALE * W_SCALE)).then_inc(silu_done, 1)

            def act_high(n, par, dst, rows, cols):
                act.wait_ge(prod_done, n + 1)
                act.copy(dst, gu[0:rows, par, 0, 0:cols]).then_inc(ahi_done, 1)

            def chunk(*job):
                silu(*job)
                act_high(*job)

            def step(i, p, half, alone, s, mlp=None, unit=None):
                if mlp:
                    silu(*mlp)
                if s["tq"] and alone:
                    act.wait_ge(qT_ps, i + 1)
                    if i >= 2:
                        act.wait_ge(xa_ps, i - 1)
                    act.copy(qT[:, p], tp_q).then_inc(qT_done, 1)
                if alone and i + 1 < PS:
                    quant_x(i + 3, seq_x(i + 1), 1 - p, True)
                if s["q"] and not alone:
                    quant_x(i + 1, seq_x(i), seq_x(i) % 2 if isinstance(i, int) else 1, alone)
                if unit:
                    w_high(*unit)
                if s["th"]:
                    act.wait_ge(x1_stored[p], 16 * half)
                    act.wait_ge(hT_ps, i - 1)
                    act.mul(h_split[:, i - 2, 0], tp_h, H_SCALE).then_inc(hhi_done, 1)
                if mlp:
                    act_high(*mlp)
                if alone and i + 1 < PS:
                    quant_ctx_pool(i + 5, i + 3)
                if s["ctx"] and not alone:
                    quant_ctx(i + 4, seq_ctx(i), 0, alone)
                if s["xa"]:
                    act.wait_ge(ln2_done, 4 * i)
                    if not isinstance(i, int) or i >= 3:
                        act.wait_ge(hT_ps, i - 2)
                        act.wait_ge(h_stored[1 - p], 16 * (half + p - 1))
                    act.activation(h_tok[:, 1 - p, :], tok[:, i - 1, :], ACT.Identity,
                                   bias=ln2[:, 1 - p, 1:2], scale=ln2[:, 1 - p, 0:1]).then_inc(h_done, 1)

            def job(m, par):
                return m, par, a_sh[:, m, 0, :], P, D

            def unit(m, slot, half):
                return m, slot, half, sw[:, m], sd[:, m], P

            w_high(*unit(0, 0, 0))
            w_high(*unit(1, 1, 0))
            act.wait_ge(scale_done, 1)
            quant_ctx_pool(1, 0)
            quant_ctx(0, 0, 0, True)
            quant_ctx(2, 1, 1, True)
            quant_ctx_pool(3, 1)
            quant_x(0, 2, 0, True)
            quant_x(1, 3, 1, True)
            quant_x(2, seq_x(0), 0, True)
            quant_ctx_pool(4, 2)
            for i in range(PS):
                step(i, i % 2, i // 2, True, stages(i))

            step(6, 0, 3, False, stages(6), None, unit(2, 0, 1))
            with act.Fori(0, 2) as r:
                for h in range(2):
                    m = 2 * r + 1 + h
                    step(m + 6, 1 - h, r + (7 + h) // 2, False, stages(m), job(m - 1, h),
                         unit(m + 2, 1 - h, r + (3 + h) // 2))
            for m in range(5, MS):
                i = m + 6
                step(i, i % 2, i // 2, False, stages(i), job(m - 1, (m - 1) % 2),
                     unit(m + 2, m % 2, (m + 2) // 2) if m + 2 < MS else None)
            step(17, 1, 8, False, stages(17), job(MS - 1, 0))
            act.wait_ge(gap_done, 1)
            act.activation(ex2[:], dlt[:], ACT.Exp, scale=1.0 / (H_SCALE * W_SCALE)).then_inc(exp_done, 1)
            act.activation(carry_a[:], tg_raw[:], ACT.Silu)
            def first_expert_unit(c):
                u = MS + c
                w_high(u, u % 2, u // 2, ew[:, 0, c], ed[:, 0, c], EC[c])

            act.wait_ge(xa_ps, NT)
            first_expert_unit(0)
            first_expert_unit(1)

            def block_chunks(b):
                n0 = block_job(b)
                with act.Fori(0, MS // 2) as r:
                    for h in range(2):
                        m = 2 * r + h
                        chunk(n0 + m, h, a_sh[:, m, 0, :], P, D)
                chunk(n0 + MS - 1, 0, a_sh[:, MS - 1, 0, :], P, D)

            block_chunks(1)
            first_expert_unit(2)

            def x_high(s, j, tpar):
                act.wait_ge(xT_ps, s + 1)
                act.mul(xe[:, 0, :, j * P:(j + 1) * P], tp_x[:, tpar], H_SCALE).then_inc(xhi_done, 1)

            def expert(e, h, r, last):
                for c in range(ME):
                    for half in range(2):
                        k = 2 * c + half
                        chunk(JOB_E + 2 * ME * e + k, k % 2, a_ex[0:EC[c], c, 0, half * HC:(half + 1) * HC],
                              EC[c], HC)
                    if not last:
                        u = MS + ME * (h + 1) + c
                        w_high(2 * ME * r + u, u % 2, ME * r + u // 2, ew[:, 1 - h, c], ed[:, 1 - h, c], EC[c])
                if not last:
                    x_high(CT * (e + 1), 0, (CT * (h + 1)) % 2)
                    x_high(CT * (e + 1) + 1, 1, (CT * (h + 1) + 1) % 2)
                if not isinstance(e, int) or e:
                    act.wait_ge(o_stored, 16 * e)
                for j in range(CT):
                    if not last and j >= 2:
                        x_high(CT * (e + 1) + j, j, (CT * (h + 1) + j) % 2)
                    act.wait_ge(o_ps, CT * e + j + 1)
                    act.mul(o_ex[:, j, :], dn[:, (CT * h + j) % 2, :], 1.0 / W_SCALE).then_inc(o_done, 1)

            for j in range(CT):
                x_high(j, j, j % 2)
            expert(0, 0, 0, False)
            with act.Fori(0, E // 2 - 1) as r:
                expert(2 * r + 1, 1, r, False)
                expert(2 * r + 2, 0, r + 1, False)
            expert(E - 1, 1, E // 2 - 1, True)
            n0 = block_job(2)
            for m in range(ME):
                chunk(n0 + m, m % 2, a_sh[:, m, 0, :], P, D)
            act.wait_ge(o_stored, 16 * E)
            with act.Fori(0, (MS - ME) // 2) as r:
                for h in range(2):
                    m = ME + 2 * r + h
                    chunk(n0 + m, 1 - h, a_sh[:, m, 0, :], P, D)
            block_chunks(3)

        @block.vector
        def _(dve):
            for t in range(NT):
                if t % TB == 0 and t:
                    dve.wait_ge(x_in[t // TB], 16)
                if t < TB:
                    dve.wait_ge(x_first[t], 16)
                dve.bn_stats(st1[:, t, :], tok[:, t, :]).then_inc(bn1, 1)
                if t % TB == TB - 1:
                    for a in range(t - TB + 1, t + 1):
                        dve.wait_ge(bn1, a + 1)
                        dve.bn_aggr(mv1[:, a, :], st1[:, a, :]).then_inc(mv1_done, 1)
            dve.wait_ge(gates_done, 1)
            dve.tensor_scalar(tgw[:], tg[:, 1:2], 1.0 / W_SCALE, None, ALU.mult).then_inc(tgw_done, 1)
            dve.wait_ge(router_hi, 1)
            dve.scalar_tensor_tensor(r_split[:, :, E:2 * E], r_raw[:], W_SCALE, r_split[:, :, 0:E],
                                     ALU.mult, ALU.subtract).then_inc(router_done, 1)
            for t in range(NT):
                dve.wait_ge(absz_done, t + 1)
                dve.tensor_reduce(zmax[:, t:t + 1], gu4[:, t % 4, :], AX.X, ALU.max).then_inc(zmax_done, 1)
                if t % TB == TB - 1:
                    b = t // TB
                    dve.wait_ge(c_in[b], 16)
                    dve.tensor_reduce(zmax[:, NT + b:NT + b + 1], ctx_raw[:, b * KD:(b + 1) * KD, :], AX.XY,
                                      ALU.max, apply_absolute_value=True).then_inc(cmax_done, 1)
            dve.wait_ge(zmax_done, NT)
            dve.tensor_reduce(amax[:, 0:1], zmax[:, 0:NT], AX.X, ALU.max).then_inc(amax_done, 1)
            dve.wait_ge(cmax_done, B)
            dve.tensor_reduce(amax[:, 1:2], zmax[:, NT:NT + B], AX.X, ALU.max).then_inc(amax_done, 1)
            dve.wait_ge(gmax_done, 1)
            dve.tensor_scalar(sc[:, 4:6], gmax[:], EPS_Q, None, ALU.max).then_inc(gmax_done, 1)
            dve.wait_ge(gmax_done, 2)
            dve.reciprocal(sc[:, 6:8], sc[:, 4:6]).then_inc(gmax_done, 1)
            dve.wait_ge(gmax_done, 3)
            dve.tensor_scalar(sc[:, 0:2], sc[:, 6:8], FP8_MAX, None, ALU.mult).then_inc(gmax_done, 1)
            dve.wait_ge(gmax_done, 4)
            dve.wait_ge(ln1_done, 4 * B)
            dve.tensor_scalar(vsc[:, 0:2, :], ln1[:, 0:2, :], sc[:, 0:1], None, ALU.mult).then_inc(scale_done, 1)
            dve.tensor_scalar(sc[:, 2:3], sc[:, 0:1], sc[:, 1:2], None, ALU.mult).then_inc(gmax_done, 1)
            dve.wait_ge(gmax_done, 5)
            dve.reciprocal(sc[:, 4:5], sc[:, 2:3]).then_inc(gmax_done, 1)
            dve.wait_ge(gmax_done, 6)
            dve.tensor_scalar(sc[:, 3:4], sc[:, 4:5], tg[:, 0:1], None, ALU.mult).then_inc(gmax_done, 1)
            def held():
                dve.tensor_copy(carry_v[:], tgw[:])

            def quant(seq, par, alone, dst):
                q_bits(seq, par)
                q_round(seq, par, alone, dst)

            def q_bits(seq, par):
                u = v20[:, par, :].bitcast(U32)
                dve.wait_ge(v20_done, seq + 1)
                dve.tensor_scalar(u, u, EXP_MASK, HALF_BIT, ALU.bitwise_and, ALU.bitwise_or).then_inc(bits_done, 1)

            def q_round(seq, par, alone, dst):
                bank, _ = v_bank(seq, alone)
                dve.wait_ge(bits_done, seq + 1)
                dve.scalar_tensor_tensor(bank, v20[:, par, :], ROUND_FLOOR, bank, ALU.max,
                                         ALU.add).then_inc(sum_done, 1)
                dve.wait_ge(sum_done, seq + 1)
                dve.scalar_tensor_tensor(dst, v20[:, par, :], ROUND_FLOOR, bank, ALU.max,
                                         ALU.subtract).then_inc(q_done, 1)

            def quant_ctx(c, seq, par, alone):
                quant(seq, par, alone, ctx_q[:, c, 0:D])

            def bits_for_pool(seq):
                u = pv[:, seq % 2, 1, :].bitcast(U32)
                dve.wait_ge(pv_done, 2 * seq + 2)
                dve.tensor_scalar(u, u, EXP_MASK, HALF_BIT, ALU.bitwise_and, ALU.bitwise_or).then_inc(pbits_done, 1)
                dve.wait_ge(pbits_done, 2 * seq + 1)
                c = pv[:, seq % 2, 1, :]
                dve.tensor_scalar(c, c, ROUND_FLOOR, None, ALU.max).then_inc(pbits_done, 1)

            def quant_x(t, tpar, seq, par, alone):
                if not isinstance(t, int) or t >= 2:
                    dve.wait_ge(qT_ps, t - 1)
                quant(seq, par, alone, q_tok[:, tpar, :])

            dve.wait_ge(gmax_done, 7)

            def prod(n, par, dst_hi, dst_lo, rows, cols):
                dve.wait_ge(silu_done, n + 1)
                dve.scalar_tensor_tensor(gu[0:rows, par, 0, 0:cols], gu[0:rows, par, 1, 0:cols],
                                         1.0 / (H_SCALE * W_SCALE), sg[0:rows, par, 0:cols], ALU.mult,
                                         ALU.mult).then_inc(prod_done, 1)

            def act_low(n, par, dst_hi, dst_lo, rows, cols):
                dve.wait_ge(ahi_done, n + 1)
                dve.tensor_tensor(dst_lo, gu[0:rows, par, 0, 0:cols], dst_hi, ALU.subtract).then_inc(alo_done, 1)

            def chunk(*job):
                prod(*job)
                act_low(*job)

            def job(n, m, par):
                return n, par, a_sh[:, m, 0, :], a_sh[:, m, 1, :], P, D

            def h_low(i):
                dve.wait_ge(hhi_done, i - 1)
                dve.scalar_tensor_tensor(h_split[:, i - 2, 1].rearrange("p k n -> p (k n)"), tp[:, 1, :],
                                         H_SCALE, h_split[:, i - 2, 0].rearrange("p k n -> p (k n)"),
                                         ALU.mult, ALU.subtract).then_inc(hlo_done, 1)

            def step(i, p, alone, s, mlp=None):
                if mlp:
                    prod(*mlp)
                if s["xa"]:
                    dve.wait_ge(xa_ps, i)
                    dve.scalar_tensor_tensor(tok[:, i - 1, :], dn[:, 0, :], sc[:, 3:4], tok[:, i - 1, :],
                                             ALU.mult, ALU.add).then_inc(x1_done, 1)
                    dve.wait_ge(x1_done, i)
                    held()
                    dve.bn_stats(st2[:, 1 - p, :], tok[:, i - 1, :]).then_inc(bn2, 1)
                    dve.wait_ge(bn2, i)
                    if not isinstance(i, int) or i >= 3:
                        dve.wait_ge(ln2_done, 4 * (i - 2))
                    held()
                    dve.bn_aggr(mv2[:, 1 - p, :], st2[:, 1 - p, :]).then_inc(mv2_done, 1)
                if s["q"] and not alone:
                    quant_x(i + 1, 1 - p, seq_x(i), seq_x(i) % 2 if isinstance(i, int) else 1, alone)
                if s["th"]:
                    h_low(i)
                if mlp:
                    act_low(*mlp)
                if s["tq"] and not alone:
                    dve.wait_ge(qT_ps, i + 1)
                    dve.wait_ge(xa_ps, i - 1)
                    dve.tensor_copy(qT[:, p], tp_q).then_inc(qT_done, 1)
                if s["ctx"] and alone:
                    bits_for_pool(i + 2)
                elif s["ctx"]:
                    quant_ctx(i + 4, seq_ctx(i), 0, alone)
                if s["q"] and alone:
                    quant_x(i + 2, p, seq_x(i), seq_x(i) % 2, alone)

            def chunk_sh(n, m, par):
                chunk(*job(n, m, par))

            bits_for_pool(0)
            quant_ctx(0, 0, 0, True)
            quant_ctx(2, 1, 1, True)
            bits_for_pool(1)
            quant_x(0, 0, 2, 0, True)
            quant_x(1, 1, 3, 1, True)
            for i in range(FIRST_CHUNK_STEP):
                step(i, i % 2, True, stages(i))
            step(6, 0, False, stages(6))
            with dve.Fori(0, 2) as r:
                for h in range(2):
                    m = 2 * r + 1 + h
                    step(m + 6, 1 - h, False, stages(m), job(m - 1, m - 1, h))
            for m in range(5, MS + 1):
                step(m + 6, m % 2, False, stages(m + 6), job(m - 1, m - 1, (m - 1) % 2))

            def y_tile(b, j):
                y = b * TB + j
                dve.wait_ge(dn_ps, y + 1)
                dst = base[:, j if b < 3 else j + TB, :]
                if b < 2:
                    dve.wait_ge(base_in[j], 16 * (b + 1))
                dve.scalar_tensor_tensor(dst, dn[:, j % 2, :], tgw[:, 0:1], dst, ALU.mult,
                                         ALU.add).then_inc(y_done, 1)

            k = [0]

            def link(ins):
                k[0] += 1
                ins.then_inc(rstep, 1)
                dve.wait_ge(rstep, k[0])

            dve.wait_ge(rt_ps, NT)
            link(dve.tensor_reduce(lg[:], tp_r.rearrange("p t (s e) -> p t e s", s=2), AX.X, ALU.add))
            for t in range(NT):
                ins = dve.max(top_v[:, t, :], lg[:, t, :])
                ins.then_inc(rstep, 1)
                k[0] += 1
            dve.wait_ge(rstep, k[0])
            for t in range(NT):
                ins = dve.max_index(top_i[:, t, :], top_v[:, t, :], lg[:, t, :])
                ins.then_inc(rstep, 1)
                k[0] += 1
            dve.wait_ge(rstep, k[0])
            dve.tensor_tensor(dlt[:], top_v[:, :, 1], top_v[:, :, 0], ALU.subtract).then_inc(gap_done, 1)
            link(dve.tensor_copy(sel[:], top_i[:, :, 0:TOPK]))
            dve.wait_ge(consts, 12)
            link(dve.tensor_tensor(
                hot[:].rearrange("p t k e -> p (t k) e"),
                sel[:].rearrange("p t k -> p (t k)").unsqueeze(2).to_broadcast([P, NT * TOPK, E]),
                iota_e[:].unsqueeze(1).to_broadcast([P, NT * TOPK, E]), ALU.is_equal))
            dve.tensor_tensor(hot_n[:], hot[:, :, 0, :], hot[:, :, 1, :], ALU.add).then_inc(cnt_ready, 1)
            for j in range(2):
                y_tile(0, j)
            dve.wait_ge(pos_ps, 1)
            for kk in range(TOPK):
                ins = dve.tensor_tensor(seat[:, :, kk, :], hot[:, :, kk, :],
                                        tp_pos.rearrange("p (t e) -> p t e", t=NT), ALU.mult)
                ins.then_inc(rstep, 1)
                k[0] += 1
            dve.wait_ge(rstep, k[0])
            link(dve.tensor_reduce(pos[:], seat[:].rearrange("p t k e -> p (t k) e"), AX.X, ALU.add))
            link(dve.tensor_scalar(valid[:], pos[:], float(CAP), None, ALU.is_lt))
            link(dve.tensor_scalar(slot_f[:], pos[:], float(CAP - 1), None, ALU.min))
            link(dve.scalar_tensor_tensor(pos[:], sel[:].rearrange("p t k -> p (t k)"), float(CAP), slot_f[:],
                                          ALU.mult, ALU.add))
            dve.tensor_copy(from_slot[:], pos[:]).then_inc(slots_done, 1)
            link(dve.tensor_scalar(slot_f[:], valid[:], -FAR, FAR, ALU.mult, ALU.add))
            dve.tensor_tensor(to_slot[:], pos[:], slot_f[:], ALU.add).then_inc(slots_done, 1)
            dve.wait_ge(exp_done, 1)
            link(dve.tensor_scalar(wsum[:], ex2[:], 1.0, None, ALU.add))
            link(dve.reciprocal(dlt[:], wsum[:]))
            link(dve.tensor_scalar(dlt[:], dlt[:], tg[:, 1:2], None, ALU.mult))
            vv = valid[:].rearrange("p (t k) -> p t k", k=TOPK)
            link(dve.tensor_tensor(wsum[:], dlt[:], ex2[:], ALU.mult))
            dve.tensor_tensor(cw[:, :, 0], dlt[:], vv[:, :, 0], ALU.mult).then_inc(weights_done, 1)
            dve.tensor_tensor(cw[:, :, 1], wsum[:], vv[:, :, 1], ALU.mult).then_inc(weights_done, 1)

            for j in range(2, TB):
                y_tile(0, j)

            n0 = block_job(1)
            with dve.Fori(0, MS // 2) as r:
                for h in range(2):
                    chunk_sh(n0 + 2 * r + h, 2 * r + h, h)
            chunk_sh(n0 + MS - 1, MS - 1, 0)
            def x_low(s, j, tpar):
                dve.wait_ge(xhi_done, s + 1)
                dve.scalar_tensor_tensor(xe[:, 1, :, j * P:(j + 1) * P], tp_x[:, tpar], H_SCALE,
                                         xe[:, 0, :, j * P:(j + 1) * P], ALU.mult,
                                         ALU.subtract).then_inc(xlo_done, 1)

            def expert(e, h, last):
                for c in range(ME):
                    for half in range(2):
                        kk = 2 * c + half
                        cols = slice(half * HC, (half + 1) * HC)
                        chunk(JOB_E + 2 * ME * e + kk, kk % 2, a_ex[0:EC[c], c, 0, cols],
                              a_ex[0:EC[c], c, 1, cols], EC[c], HC)
                if not last:
                    for j in range(CT):
                        x_low(CT * (e + 1) + j, j, (CT * (h + 1) + j) % 2)

            for j in range(TB):
                x_low(j, j, j % 2)
                y_tile(1, j)
            x_low(TB, TB, TB % 2)
            expert(0, 0, False)
            with dve.Fori(0, E // 2 - 1) as r:
                expert(2 * r + 1, 1, False)
                expert(2 * r + 2, 0, False)
            expert(E - 1, 1, True)

            dve.wait_ge(weights_done, 2)

            def combine(q, t, p, half, place, ring):
                if not ring:
                    dve.wait_ge(cbase_in, 16 * NT // 2)
                if ring:
                    dve.wait_ge(cring_in[p], 16 * (half - 3))
                dve.wait_ge(cg_in[p], 32 * (half + 1))
                dst = base[:, place, :]
                w = cw[:].rearrange("p t k -> p (t k)")
                dve.scalar_tensor_tensor(dst, comb[:, p, 0, :], w[:, bass.ds(TOPK * t, 1)], dst, ALU.mult,
                                         ALU.add).then_inc(c1_done, 1)
                dve.wait_ge(c1_done, q + 1)
                dve.scalar_tensor_tensor(dst, comb[:, p, 1, :], w[:, bass.ds(TOPK * t + 1, 1)], dst, ALU.mult,
                                         ALU.add).then_inc(c_done, 1)

            n0 = block_job(2)
            for m in range(2):
                chunk_sh(n0 + m, m, m)
            with dve.Fori(0, 4) as r:
                for h in range(2):
                    q = 2 * r + h
                    chunk_sh(n0 + q + 2, q + 2, h)
                    combine(q, q + 8, h, r, q, False)
            chunk_sh(n0 + MS - 1, MS - 1, 0)
            combine(8, 0, 0, 4, 8, True)
            for j in range(TB):
                y_tile(2, j)
            n0 = block_job(3)
            for m in range(7):
                q = 9 + m
                chunk_sh(n0 + m, m, m % 2)
                combine(q, q - 8, q % 2, q // 2, 8 + q % 2, True)
            for m in range(7, MS):
                chunk_sh(n0 + m, m, m % 2)
            for j in range(TB):
                y_tile(3, j)

        @block.tensor
        def _(pe):
            pe.wait_ge(consts, 12)

            def transpose_q(i, p):
                pe.wait_ge(q_done, x_ready(i))
                if not isinstance(i, int) or i >= 1:
                    pe.wait_ge(qT_done, i)
                for k in range(KD):
                    ins = pe.transpose(tp_q[:, k, :], q_tok[:, p, k * P:(k + 1) * P], id_b[:])
                ins.then_inc(qT_ps, 1)

            def step(i, p, s):
                early = isinstance(i, int) and i < PS
                if s["xa"]:
                    pe.wait_ge(qT_done, i)
                    if isinstance(i, int) and i < PS + 2:
                        pe.wait_ge(pq_done, i + 1)
                    else:
                        pe.wait_ge(q_done, seq_ctx(min(i - 2, LAST_CTX_STEP) if isinstance(i, int) else i - 2) + 1)
                    if not isinstance(i, int) or i >= 2:
                        pe.wait_ge(x1_done, i - 1)
                    if isinstance(i, int) and i == 1:
                        pe.wait_ge(mask_in, 48)
                    b = (i - 1) // TB
                    for k in range(KD):
                        pe.matmul(dn[:, 0, :], qT[:, 1 - p, k, :], ctx_q[:, TB * b + k, 0:D], start=k == 0,
                                  stop=False)
                    pe.matmul(dn[:, 0, :], pick[:, b, :], mask_p[:], start=False, stop=True).then_inc(xa_ps, 1)
                if s["tq"] and early:
                    transpose_q(i, p)
                if s["th"]:
                    pe.wait_ge(h_done, i - 1)
                    if not isinstance(i, int) or i >= 3:
                        pe.wait_ge(hlo_done, i - 2)
                    for k in range(KD):
                        ins = pe.transpose(tp_h[:, k, :], h_tok[:, p, k * P:(k + 1) * P], id_f[:])
                    ins.then_inc(hT_ps, 1)
                if s["rt"]:
                    pe.wait_ge(hlo_done, i - 2)
                    pe.wait_ge(qT_done, min(i + early, NT) if isinstance(i, int) else i)
                    if isinstance(i, int) and i == 3:
                        pe.wait_ge(router_done, 1)
                    for k in range(KD):
                        for part in range(2):
                            ins = pe.matmul(tp_r[:, i - 3, :], h_split[:, i - 3, part, k, :], r_split[:, k, :],
                                            start=k + part == 0, stop=k + part == KD)
                    ins.then_inc(rt_ps, 1)
                if s["tq"] and not early:
                    transpose_q(i, p)

            def chunk_sh(n, b, m, par, free):
                if free is not None:
                    pe.wait_ge(alo_done, free)
                for g in range(2):
                    for k in range(KD):
                        for w, a in PARTS:
                            ins = pe.matmul(gu[:, par, g, :], sw[:, m, w, k, g, :],
                                            h_split[:, b * TB:(b + 1) * TB, a, k, :],
                                            start=k + w + a == 0, stop=k == KD - 1 and w == 1)
                ins.then_inc(gu_ps, 1)

            def down_sh(n0, y, j, par, wait):
                if wait:
                    pe.wait_ge(y_done, y - 1)
                for m in range(MS):
                    if m == 0:
                        pe.wait_ge(alo_done, n0 + MS - 1)
                    if m == MS - 1:
                        pe.wait_ge(alo_done, n0 + MS)
                    for w, a in PARTS:
                        ins = pe.matmul(dn[:, par, :], a_sh[:, m, a, bass.ds(j * P, P)], sd[:, m, w, :],
                                        start=m + w + a == 0, stop=m == MS - 1 and w == 1)
                ins.then_inc(dn_ps, 1)

            def block_chunks(b):
                n0 = block_job(b)
                chunk_sh(n0, b, 0, 0, n0)
                chunk_sh(n0 + 1, b, 1, 1, n0)
                with pe.Fori(1, MS // 2) as r:
                    for h in range(2):
                        m = 2 * r + h
                        chunk_sh(n0 + m, b, m, h, n0 + m - 1)
                chunk_sh(n0 + MS - 1, b, MS - 1, 0, n0 + MS - 2)

            def block_down(b):
                with pe.Fori(0, TB // 2) as r:
                    for h in range(2):
                        j = 2 * r + h
                        down_sh(block_job(b), b * TB + j, j, h, True)

            for i in range(FIRST_CHUNK_STEP):
                step(i, i % 2, stages(i))
            pe.wait_ge(q_done, seq_x(FIRST_CHUNK_STEP - 1) + 1)
            pe.wait_ge(hlo_done, TB)
            for m in range(2):
                step(m + 6, m, stages(m + 6))
                pe.wait_ge(wlo_done, 2 * m + 2)
                chunk_sh(m, 0, m, m, None)
            with pe.Fori(1, 3) as r:
                for h in range(2):
                    m = 2 * r + h
                    step(m + 6, h, stages(m))
                    pe.wait_ge(wlo_done, 2 * m + 2)
                    chunk_sh(m, 0, m, h, m - 1)
            for m in range(6, MS):
                step(m + 6, m % 2, stages(m + 6))
                pe.wait_ge(wlo_done, 2 * m + 2)
                chunk_sh(m, 0, m, m % 2, m - 1)
            step(NT + 1, 1, stages(NT + 1))
            step(NT + 2, 0, stages(NT + 2))
            pe.wait_ge(x1_done, NT)
            pe.wait_ge(q_done, x_ready(NT - 1))
            for j in range(2):
                down_sh(0, j, j, j % 2, False)

            pe.wait_ge(cnt_ready, 1)
            pe.wait_ge(hlo_done, NT)
            counts = hot_n[:].rearrange("p t e -> p (t e)")
            pe.matmul(tp_pos, before[:], counts, start=True, stop=False)
            for t in range(1, NT):
                ins = pe.matmul(tp_pos[:, t * E:NT * E], ones_b[:], counts[:, 0:(NT - t) * E], start=False,
                                stop=t == NT - 1)
            ins.then_inc(pos_ps, 1)
            for j in range(2, TB):
                down_sh(0, j, j, j % 2, True)

            block_chunks(1)

            def transposes(s, j, par):
                if not isinstance(s, int) or s >= 2:
                    pe.wait_ge(xlo_done, s - 1)
                for k in range(KD):
                    ins = pe.transpose(tp_x[:, par, k, :], grow[:, j, k * P:(k + 1) * P], id_f[:])
                ins.then_inc(xT_ps, 1)

            pe.wait_ge(g_in, 16 * CT)
            for j in range(TB):
                transposes(j, j, j % 2)
                down_sh(block_job(1), TB + j, j, j % 2, True)
            transposes(TB, TB, TB % 2)

            def expert(e, h, last):
                n0 = JOB_E + 2 * ME * e
                pe.wait_ge(xlo_done, CT * (e + 1))
                for c in range(ME):
                    pe.wait_ge(wlo_done, 2 * (MS + ME * e + c + 1))
                    for half in range(2):
                        k6 = 2 * c + half
                        pe.wait_ge(alo_done, n0 + k6 - 1 if not (isinstance(e, int) and e == 0 and k6 < 2) else JOB_E)
                        for g in range(2):
                            for k in range(KD):
                                for w, a in PARTS:
                                    ins = pe.matmul(gu[0:EC[c], k6 % 2, g, 0:HC], ew[:, h, c, w, k, g, 0:EC[c]],
                                                    xe[:, a, k, half * HC:(half + 1) * HC],
                                                    start=k + w + a == 0, stop=k == KD - 1 and w == 1)
                        ins.then_inc(gu_ps, 1)
                if not last:
                    pe.wait_ge(g_in, 16 * CT * (e + 2))
                    transposes(CT * (e + 1), 0, (CT * (1 - h)) % 2)
                    transposes(CT * (e + 1) + 1, 1, (CT * (1 - h) + 1) % 2)
                def down(j, chunks):
                    for c in chunks:
                        for w, a in PARTS:
                            ins = pe.matmul(dn[:, (CT * h + j) % 2, :], a_ex[0:EC[c], c, a, j * P:(j + 1) * P],
                                            ed[0:EC[c], h, c, w, :], start=c + w + a == 0,
                                            stop=c == ME - 1 and w == 1)
                    return ins

                if isinstance(e, int) and e == 0:
                    pe.wait_ge(y_done, 2 * TB)
                else:
                    pe.wait_ge(o_done, CT * e)
                pe.wait_ge(alo_done, n0 + 2 * ME - 2)
                for j in range(2):
                    down(j, range(ME - 1))
                pe.wait_ge(alo_done, n0 + 2 * ME)
                for j in range(2):
                    down(j, [ME - 1]).then_inc(o_ps, 1)
                for j in range(2, CT):
                    if not last:
                        transposes(CT * (e + 1) + j, j, (CT * (1 - h) + j) % 2)
                    pe.wait_ge(o_done, CT * e + j - 1)
                    down(j, range(ME)).then_inc(o_ps, 1)

            expert(0, 0, False)
            with pe.Fori(0, E // 2 - 1) as r:
                expert(2 * r + 1, 1, False)
                expert(2 * r + 2, 0, False)
            expert(E - 1, 1, True)

            for b in (2, 3):
                block_chunks(b)
                if b == 2:
                    pe.wait_ge(o_done, CT * E)
                block_down(b)


_INS = ["x", "ctx_2048", "mask_Bx1xS2_ff0", "g_xattn", "g_ffn", "L0_ffn_router", "L0_ffn_w_up_gate",
        "L0_ffn_w_down", "L0_ffn_shared_w_up_gate", "L0_ffn_shared_w_down"]


def kernel(**inputs):
    import numpy as np
    import concourse.bacc as bacc
    from concourse.bass_utils import run_bass_kernel_spmd

    nc = bacc.Bacc("TRN2", target_bir_lowering=False, num_devices=1)
    arrays, args = {}, []
    for name in _INS:
        a = np.ascontiguousarray(inputs[name])
        arrays[f"in_{name}"] = a
        args.append(nc.dram_tensor(f"in_{name}", a.shape, mybir.dt.from_np(a.dtype), kind="ExternalInput").ap())
    shape = arrays["in_x"].shape
    args.append(nc.dram_tensor("out_0", shape, F32, kind="ExternalOutput").ap())
    build_flamingo(nc, *args)
    r = run_bass_kernel_spmd(nc, [arrays], core_ids=[0])
    return r.results[0]["out_0"]
```

```python
from contextlib import ExitStack

import concourse.bass as bass
from concourse import mybir

ALU = mybir.AluOpType
ACT = mybir.ActivationFunctionType
AX = mybir.AxisListType
F32 = mybir.dt.float32
F16 = mybir.dt.float16
BF16 = mybir.dt.bfloat16
U32 = mybir.dt.uint32

P = 128
EPS_LN = 1e-5
EPS_Q = 1e-12
FP8_MAX = 448.0
H_SCALE = 2.0 ** 8
W_SCALE = 2.0 ** 6
ROUND_UP = 2.0 ** 20
ROUND_FLOOR = 1.5 * 2.0 ** 14
EXP_MASK = 0x7F800000
HALF_BIT = 0x00400000
PARTS = ((0, 0), (0, 1), (1, 0))
FAR = 1.0e6


def build_flamingo(nc, x, ctx_in, mask, g_x, g_f, router, w_ug, w_dn, sw_ug, sw_dn, out):
    B, S, D = x.shape
    E, _, I2 = w_ug.shape
    I = I2 // 2
    J = sw_dn.shape[0]
    T = B * S
    NT = T // P
    TB = S // P
    KD = D // P
    MS = J // P
    ME = -(-I // P)
    EC = [min(P, I - c * P) for c in range(ME)]
    TOPK = 2
    CAP = -(-T * TOPK * 5 // (E * 4))
    CT = CAP // P
    HC = CAP // 2
    UNIT = KD * 2 * P + D
    UW = KD * 2 * P
    FIRST_CHUNK_STEP = TB + 1
    assert T == 2048 and D == 512 and CT * P == CAP and MS == 11 and ME == 3 and TB == 4

    x1_dram = nc.dram_tensor("x1_scratch", (T, D), F32, kind="Internal").ap()
    h_dram = nc.dram_tensor("h_scratch", (T, D), F32, kind="Internal").ap()
    mask_dram = nc.dram_tensor("mask_scratch", (3, B * D), BF16, kind="Internal").ap()
    slot_dram = nc.dram_tensor("slot_scratch", (E * CAP, 1), U32, kind="Internal").ap()
    eo_dram = nc.dram_tensor("expert_out_scratch", (E * CAP, D), F32, kind="Internal").ap()

    es = ExitStack()
    with es:
        def sb(name, shape, dt):
            return es.enter_context(nc.sbuf_tensor(name, shape, dt))

        def sem(name):
            return es.enter_context(nc.semaphore(name))

        tok = sb("tok", [P, NT, D], F32)
        h_split = tok[:].rearrange("p t d -> p (t d)").bitcast(F16).rearrange(
            "p (t s k n) -> p t s k n", t=NT, s=2, k=KD)
        xe = tok[:, 0:CT, :].rearrange("p t d -> p (t d)").bitcast(F16).rearrange(
            "p (s k n) -> p s k n", s=2, k=KD)
        sw = sb("sw", [P, MS, 2, KD, 2, P], F16)
        sd = sb("sd", [P, MS, 2, D], F16)
        act_reg = sb("act_reg", [P, MS * 2 * D], F16)
        a_sh = act_reg[:].rearrange("p (m s n) -> p m s n", m=MS, s=2)
        a_ex = act_reg[:, 0:ME * 2 * CAP].rearrange("p (m s n) -> p m s n", m=ME, s=2)
        o_ex = act_reg[:, ME * 2 * CAP:ME * 2 * CAP + CT * D * 2].bitcast(F32).rearrange(
            "p (j d) -> p j d", j=CT)
        n_ew = 2 * ME * 2 * KD * 2 * P
        n_ed = 2 * ME * 2 * D
        ewr = sb("expert_w", [P, n_ew + n_ed], F16)
        ew = ewr[:, 0:n_ew].rearrange("p (b m s k g n) -> p b m s k g n", b=2, m=ME, s=2, k=KD, g=2)
        ed = ewr[:, n_ew:n_ew + n_ed].rearrange("p (b m s n) -> p b m s n", b=2, m=ME, s=2)
        ctx_raw = ewr[:, 0:B * KD * D * 2].bitcast(F32).rearrange("p (c n) -> p c n", c=B * KD)
        ctx_q = ewr[:, 0:B * KD * D * 2].bitcast(BF16).rearrange("p (c n) -> p c n", c=B * KD)
        pv = sw[:, MS - 2:MS].rearrange("p m s k g n -> p (m s k g n)").bitcast(F32).rearrange("p (b s n) -> p b s n", b=2, s=2)
        grow = sb("gathered", [P, CT, D], F32)
        v20 = grow[:, 0:2, :]
        h_tok = grow[:, 2:4, :]
        q_tok = grow[:, 4, :].bitcast(BF16).rearrange("p (b d) -> p b d", b=2)
        comb = grow[:, 0:4, :].rearrange("p (b k) d -> p b k d", b=2)
        base = sb("base", [P, 4 + 2 * UNIT // D, D], F32)
        raw = base[:, 4:4 + 2 * UNIT // D, :].rearrange("p a d -> p (a d)").rearrange(
            "p (b u) -> p b u", b=2)
        sg = sb("silu_gate", [P, 2, D], F32)
        qT = sb("qT", [P, 2, KD, P], BF16)
        id_f = sb("ident_f32", [P, P], F32)
        id_b = sb("ident_bf16", [P, P], BF16)
        before = sb("before", [P, P], BF16)
        ones_b = sb("ones_bf16", [P, P], BF16)
        MC = B * D // P
        mask_raw = sb("mask_raw", [P, MC], F32)
        mask_res = sb("mask_rest", [P, 3, MC], F32)
        mask_b = sb("mask_parts", [P, 3, MC], BF16)
        mask_p = sb("mask_stack", [3 * B, D], BF16)
        pick = sb("pick_batch", [3 * B, B, P], BF16)
        r_raw = sb("router_raw", [P, KD, E], F32)
        r_split = sb("router_split", [P, KD, 2 * E], F16)
        tg = sb("tanh_gates", [P, 2], F32)
        tg_raw = sb("gates_raw", [P, 2], F32)
        tgw = sb("ffn_gate_scaled", [P, 1], F32)
        carry_a = sb("carry_a", [P, 2], F32)
        carry_v = sb("carry_v", [P, 1], F32)
        carry_p = sb("carry_p", [P, 3], F32)
        st1 = sb("stats1", [P, NT, 6], F32)
        mv1 = sb("meanvar1", [P, NT, 2], F32)
        ln1 = sb("rstd_shift1", [P, 4, NT], F32)
        nhalf = sb("minus_half", [P, NT], F32)
        zmax = sb("zmax", [P, NT + B], F32)
        amax = sb("amax", [P, 2], F32)
        gmax = sb("gmax", [P, 2], F32)
        sc = sb("scales", [P, 8], F32)
        vsc = sb("quant_scale", [P, 2, NT], F32)
        st2 = sb("stats2", [P, 2, 6], F32)
        mv2 = sb("meanvar2", [P, 2, 2], F32)
        ln2 = sb("rstd_shift2", [P, 2, 4], F32)
        lg = sb("logits", [P, NT, E], F32)
        top_v = sb("top_values", [P, NT, E], F32)
        top_i = sb("top_index", [P, NT, E], U32)
        sel = sb("expert_of", [P, NT, TOPK], F32)
        hot = sb("one_hot", [P, NT, TOPK, E], F32)
        hot_n = sb("count_rows", [P, NT, E], BF16)
        seat = sb("seat_products", [P, NT, TOPK, E], F32)
        pos = sb("position", [P, NT * TOPK], F32)
        valid = sb("valid", [P, NT * TOPK], F32)
        slot_f = sb("slot_f", [P, NT * TOPK], F32)
        to_slot = sb("scatter_slot", [P, NT * TOPK], U32)
        from_slot = sb("gather_slot", [P, NT * TOPK], U32)
        dlt = sb("logit_gap", [P, NT], F32)
        ex2 = sb("exp_gap", [P, NT], F32)
        wsum = sb("weight_sum", [P, NT], F32)
        cw = sb("combine_w", [P, NT, TOPK], F32)
        iota_e = sb("iota_e", [P, E], F32)
        tok_id = sb("token_id", [P, NT], U32)
        zero_i = sb("zero_slots", [P, E * CT], U32)
        slot_tok = sb("slot_token", [P, E, CT], U32)

        gu = es.enter_context(nc.psum_tensor("gu", [P, 2, 2, D], F32))
        gu4 = gu[:].rearrange("p a g n -> p (a g) n")
        dn = es.enter_context(nc.psum_tensor("dn", [P, 2, D], F32))
        tp = es.enter_context(nc.psum_tensor("tp", [P, 2, D], F32))
        tp_q = tp[:, 0, 0:D // 2].bitcast(BF16).rearrange("p (k n) -> p k n", k=KD)
        tp_h = tp[:, 1, :].rearrange("p (k n) -> p k n", k=KD)
        tp_r = tp[:, 0, D // 2:D].rearrange("p (t c) -> p t c", t=NT)
        tp_x = tp[:].rearrange("p b (k n) -> p b k n", k=KD)
        tp_pos = tp[:, 1, 0:NT * E]

        x_first = [sem(f"x_first{t}") for t in range(2 * TB)]
        x_in = [sem(f"x_in{b}") for b in range(2, B)]
        c_in = [sem(f"c_in{b}") for b in range(B)]
        small_in = sem("small_in")
        consts = sem("consts")
        zero_done = sem("zero_done")
        table_zeroed = sem("table_zeroed")
        gates_done = sem("gates_done")
        tgw_done = sem("tgw_done")
        router_hi = sem("router_hi")
        router_done = sem("router_done")
        mask_done = sem("mask_done")
        mask_out = sem("mask_stored")
        mask_in = sem("mask_in")
        bn1 = sem("bn1")
        mv1_done = sem("mv1_done")
        ln1_done = sem("ln1_done")
        absz_done = sem("absz_done")
        zmax_done = sem("zmax_done")
        cmax_done = sem("cmax_done")
        pv_done = sem("pool_v_done")
        pbits_done = sem("pool_bits_done")
        pround = sem("pool_round_steps")
        pq_done = sem("pool_q_done")
        amax_done = sem("amax_done")
        gmax_done = sem("gmax_done")
        scale_done = sem("scale_done")
        v_done = sem("v_done")
        v20_done = sem("v20_done")
        bits_done = sem("bits_done")
        sum_done = sem("sum_done")
        q_done = sem("q_done")
        qT_ps = sem("qT_in_psum")
        qT_done = sem("qT_done")
        xa_ps = sem("attn_in_psum")
        x1_done = sem("x1_done")
        bn2 = sem("bn2")
        mv2_done = sem("mv2_done")
        ln2_done = sem("ln2_done")
        h_done = sem("h_done")
        x1_stored = [sem(f"x1_stored{i}") for i in range(2)]
        h_stored = [sem(f"h_stored{i}") for i in range(2)]
        hT_ps = sem("hT_in_psum")
        hhi_done = sem("h_hi_done")
        hlo_done = sem("h_lo_done")
        rt_ps = sem("logits_in_psum")
        raw_in = [sem(f"raw_in{i}") for i in range(2)]
        whi_done = sem("w_hi_done")
        wsc_done = sem("w_scaled")
        wlo_done = sem("w_lo_done")
        gu_ps = sem("gate_up_in_psum")
        silu_done = sem("silu_done")
        prod_done = sem("product_done")
        ahi_done = sem("act_hi_done")
        alo_done = sem("act_lo_done")
        dn_ps = sem("down_in_psum")
        base_in = [sem(f"base_in{i}") for i in range(TB)]
        y_done = sem("y_done")
        y_stored = [sem(f"y_stored{i}") for i in range(2)]
        rstep = sem("routing_steps")
        cnt_ready = sem("counts_ready")
        pos_ps = sem("positions_in_psum")
        gap_done = sem("gap_done")
        exp_done = sem("exp_done")
        slots_done = sem("slots_done")
        weights_done = sem("combine_weights_done")
        scattered = sem("scattered")
        table_in = sem("table_in")
        g_in = sem("gathered_in")
        xT_ps = sem("xT_in_psum")
        xhi_done = sem("x_hi_done")
        xlo_done = sem("x_lo_done")
        o_ps = sem("expert_out_in_psum")
        o_done = sem("expert_out_done")
        o_stored = sem("expert_out_stored")
        cbase_in = sem("comb_base_in")
        cring_in = [sem(f"comb_ring_in{i}") for i in range(2)]
        cg_in = [sem(f"comb_rows_in{i}") for i in range(2)]
        c1_done = sem("comb_first_done")
        c_done = sem("comb_done")
        out_stored = [sem(f"out_stored{i}") for i in range(2)]

        NQC = B * KD
        LAST_CTX_STEP = NQC - 5
        PS = FIRST_CHUNK_STEP + 1

        def seq_ctx(i):
            return 4 + PS + 2 * (i - PS)

        def seq_x(i):
            if isinstance(i, int) and i < PS:
                return 3 + i
            return seq_ctx(i) - 1 if not isinstance(i, int) or i <= LAST_CTX_STEP else \
                seq_ctx(LAST_CTX_STEP) + i - LAST_CTX_STEP

        def x_ready(t):
            return 1 if isinstance(t, int) and t == 0 else seq_x(t - 1) + 1

        def pool_seq(c):
            return c // 2 if c < KD else c - 2

        C_ROUND = ((), (4,), (5,), (6, 7), (8,), (9,))
        X_AHEAD = ((1, 2), (3,), (4,), (5,), (6,), ())
        C_AHEAD = ((4,), (5,), (6,), (7,), (8, 9), ())

        JOB_E = 2 * MS
        JOB_2 = JOB_E + 2 * ME * E

        def block_job(b):
            return b * MS if b < 2 else JOB_2 + (b - 2) * MS

        NU = MS + E * ME

        x_v = x.rearrange("b (j p) d -> b p j d", p=P)
        c_v = ctx_in.rearrange("b (k p) n -> b p k n", p=P)
        x1_v = x1_dram.rearrange("(t p) d -> p t d", p=P)
        h_v = h_dram.rearrange("(t p) d -> p t d", p=P)
        out_v = out.rearrange("b (j p) d -> p (b j) d", p=P)
        swv = sw_ug.rearrange("(k p) (g m n) -> p m k g n", p=P, g=2, n=P)
        sdv = sw_dn.rearrange("(m p) d -> p m d", p=P)
        ewv = w_ug.rearrange("e (k p) (g n) -> p e k g n", p=P, g=2)
        table_v = slot_dram.rearrange("(e p j) o -> p e (j o)", p=P, j=CT)
        eo_v = eo_dram.rearrange("(e p j) d -> p e (j d)", p=P, j=CT)

        block = es.enter_context(nc.Block())

        def raw_w(slot, cols):
            return raw[:, slot, 0:UW].rearrange("p (k g n) -> p k g n", k=KD, g=2)[:, :, :, 0:cols]

        def raw_d(slot, rows):
            return raw[0:rows, slot, UW:UNIT]

        def stages(i):
            if not isinstance(i, int):
                return dict(q=True, ctx=True, tq=True, xa=True, th=True, rt=True)
            return dict(q=i < NT - 1, ctx=i <= LAST_CTX_STEP, tq=i < NT, xa=1 <= i <= NT,
                        th=2 <= i <= NT + 1, rt=3 <= i <= NT + 2)

        def v_bank(seq, alone):
            return (gu4[:, (seq + 3) % 4, :], 4) if alone else (dn[:, 1, :], 1)

        @block.sync
        def _(sp):
            def load_unit_shared(m, slot, half, first=False):
                if not first:
                    sp.wait_ge(wlo_done, 2 * (2 * half + slot - 1))
                sp.dma_start(raw[:, slot, 0:UW].rearrange("p (k g n) -> p k g n", k=KD, g=2)[:, :, 0, :],
                             swv[:, m, :, 0, :]).then_inc(raw_in[slot], 16)
                sp.dma_start(raw[:, slot, 0:UW].rearrange("p (k g n) -> p k g n", k=KD, g=2)[:, :, 1, :],
                             swv[:, m, :, 1, :]).then_inc(raw_in[slot], 16)
                sp.dma_start(raw_d(slot, P), sdv[:, m, :]).then_inc(raw_in[slot], 16)

            def load_unit_expert(e, c, slot, half):
                sp.wait_ge(wlo_done, 2 * (2 * half + slot - 1))
                n = EC[c]
                for g in range(2):
                    sp.dma_start(raw_w(slot, n)[:, :, g, :],
                                 ewv[:, e, :, g, c * P:c * P + n]).then_inc(raw_in[slot], 16)
                sp.dma_start(raw_d(slot, n), w_dn[e, c * P:c * P + n, :]).then_inc(raw_in[slot], 16)

            def store_tile(t, par):
                sp.wait_ge(x1_done, t + 1)
                sp.dma_start(x1_v[:, t, :], tok[:, t, :]).then_inc(x1_stored[par], 16)
                sp.wait_ge(h_done, t + 1)
                sp.dma_start(h_v[:, t, :], h_tok[:, par, :]).then_inc(h_stored[par], 16)

            for t in range(2 * TB):
                sp.dma_start(tok[:, t, :], x_v[t // TB][:, t % TB, :]).then_inc(x_first[t], 16)
            for b in range(2, B):
                sp.dma_start(tok[:, b * TB:(b + 1) * TB, :], x_v[b]).then_inc(x_in[b - 2], 16)
            sp.dma_start(tg_raw[:, 0:1], g_x.rearrange("(a o) -> a o", o=1).to_broadcast([P, 1])).then_inc(small_in, 16)
            sp.dma_start(tg_raw[:, 1:2], g_f.rearrange("(a o) -> a o", o=1).to_broadcast([P, 1])).then_inc(small_in, 16)
            sp.dma_start(mask_raw[:], mask.rearrange("b o (i n) -> (b o i) n", n=MC)).then_inc(small_in, 16)
            sp.dma_start(r_raw[:], router.rearrange("(k p) e -> p k e", p=P)).then_inc(small_in, 16)
            for b in range(B):
                sp.dma_start(ctx_raw[:, b * KD:(b + 1) * KD, :], c_v[b]).then_inc(c_in[b], 16)
            load_unit_shared(0, 0, 0, first=True)
            load_unit_shared(1, 1, 0, first=True)
            sp.wait_ge(zero_done, 1)
            sp.dma_start(table_v, zero_i[:].rearrange("p (e j) -> p e j", e=E)).then_inc(table_zeroed, 16)

            sp.wait_ge(mask_done, 6)
            sp.dma_start(mask_dram.rearrange("a (p n) -> p a n", n=MC), mask_b[:]).then_inc(mask_out, 16)
            sp.wait_ge(mask_out, 16)
            sp.dma_start(mask_p[:], mask_dram.rearrange("a (b d) -> (a b) d", b=B)).then_inc(mask_in, 16)

            for i in range(1, 6):
                store_tile(i - 1, (i - 1) % 2)
                if i == 5:
                    load_unit_shared(2, 0, 1)
            load_unit_shared(3, 1, 1)
            with sp.Fori(0, 3) as r:
                for h in range(2):
                    store_tile(5 + 2 * r + h, (5 + h) % 2)
                    load_unit_shared(4 + 2 * r + h, h, r + 2)
            def load_base(b, j):
                y = b * TB + j
                if b:
                    sp.wait_ge(y_stored[j % 2], 16 * (2 * b))
                sp.dma_start(base[:, j, :], x1_v[:, y, :]).then_inc(base_in[j], 16)

            for i in range(12, 17):
                if i == 13:
                    for par in range(2):
                        sp.wait_ge(x1_stored[par], 16 * 6)
                    for j in range(TB):
                        load_base(0, j)
                store_tile(i - 1, (i - 1) % 2)
                if i == 12:
                    load_unit_shared(10, 0, 5)

            def load_expert_unit_after(u):
                e, c = divmod(u - MS, ME)
                load_unit_expert(e, c, u % 2, u // 2)

            def store_y(b, j):
                sp.wait_ge(y_done, b * TB + j + 1)
                sp.dma_start(x1_v[:, b * TB + j, :], base[:, j, :]).then_inc(y_stored[j % 2], 16)

            for u in (MS, MS + 1):
                load_expert_unit_after(u)
            for par in range(2):
                sp.wait_ge(x1_stored[par], 16 * NT // 2)
                sp.wait_ge(h_stored[par], 16 * NT // 2)
            for j in range(TB):
                store_y(0, j)
            for j in range(TB):
                load_base(1, j)
            sp.wait_ge(scattered, 16 * NT * TOPK)
            sp.dma_start(slot_tok[:], table_v).then_inc(table_in, 16)
            load_expert_unit_after(MS + 2)
            load_expert_unit_after(MS + 3)
            for j in range(TB):
                store_y(1, j)
            load_expert_unit_after(MS + 4)

            def store_expert(e):
                sp.wait_ge(o_done, CT * (e + 1))
                sp.dma_start(eo_v[:, e, :], o_ex.rearrange("p j d -> p (j d)")).then_inc(o_stored, 16)

            def expert_step(e, h, r, last=False):
                for c in range(ME):
                    k = MS + ME * (h + 1) + c + 2
                    if isinstance(r, int) and k + 2 * ME * r >= NU:
                        continue
                    cc = (c + 2) % ME
                    load_unit_expert(e + 1 + (c + 2) // ME, cc, k % 2, r * ME + k // 2)
                store_expert(e)

            for par in range(2):
                sp.wait_ge(y_stored[par], 16 * TB)
            for q in range(TB):
                sp.dma_start(base[:, q, :], x1_v[:, 8 + q, :]).then_inc(cbase_in, 16)
            with sp.Fori(0, E // 2 - 1) as r:
                for h in range(2):
                    expert_step(2 * r + h, h, r)
            for h in range(2):
                expert_step(E - 2 + h, h, E // 2 - 1)

            sp.wait_ge(wlo_done, 2 * NU)
            for q in range(TB, 8):
                sp.dma_start(base[:, q, :], x1_v[:, 8 + q, :]).then_inc(cbase_in, 16)
            for q in range(8, 16):
                if q >= 10:
                    sp.wait_ge(c_done, q - 1)
                    sp.dma_start(out_v[:, q - 10, :], base[:, q % 2 + 8, :]).then_inc(out_stored[q % 2], 16)
                    sp.wait_ge(out_stored[q % 2], 16 * ((q - 8) // 2))
                sp.dma_start(base[:, q % 2 + 8, :], x1_v[:, q - 8, :]).then_inc(cring_in[q % 2], 16)
            for q in range(14, 16):
                sp.wait_ge(c_done, q + 1)
                sp.dma_start(out_v[:, q - 8, :], base[:, q % 2 + 8, :]).then_inc(out_stored[q % 2], 16)
            for j in range(2 * TB):
                sp.wait_ge(y_done, 2 * TB + j + 1)
                sp.dma_start(out_v[:, 2 * TB + j, :], base[:, j, :]).then_inc(out_stored[j % 2], 16)
            for par in range(2):
                sp.wait_ge(out_stored[par], 16 * NT // 2)

        @block.gpsimd
        def _(pool):
            pool.memset(zero_i[:], 0).then_inc(zero_done, 1)
            pool.memset(id_f[:], 0.0).then_inc(consts, 1)
            pool.memset(ones_b[:], 1.0).then_inc(consts, 1)
            pool.memset(nhalf[:], -0.5).then_inc(consts, 1)
            pool.memset(pick[:], 0.0).then_inc(consts, 1)
            pool.iota(tok_id[:], pattern=[[P, NT]], base=0, channel_multiplier=1).then_inc(consts, 1)
            pool.iota(iota_e[:], pattern=[[1, E]], base=0, channel_multiplier=0,
                      allow_small_or_imprecise_dtypes=True).then_inc(consts, 1)
            pool.wait_ge(consts, 6)
            pool.affine_select(out=id_f[:], in_=id_f[:], pattern=[[-1, P]], compare_op=ALU.not_equal,
                               fill=1.0, base=0, channel_multiplier=1).then_inc(consts, 1)
            pool.affine_select(out=before[:], in_=ones_b[:], pattern=[[1, P]], compare_op=ALU.is_gt,
                               fill=0.0, base=0, channel_multiplier=-1).then_inc(consts, 1)
            for a in range(3):
                pool.affine_select(out=pick[:], in_=pick[:], pattern=[[-1, B], [0, P]], compare_op=ALU.not_equal,
                                   fill=1.0, base=-a * B, channel_multiplier=1).then_inc(consts, 1)
                pool.wait_ge(consts, 9 + a)
            pool.tensor_copy(id_b[:], id_f[:]).then_inc(consts, 1)

            def held(col=0):
                pool.tensor_tensor(carry_p[:, col:col + 1], nhalf[:, 0:1], nhalf[:, 1:2], ALU.add)

            def rstd_shift(mean, var, tmp, rstd, neg, shift, n, s, k0):
                held()
                pool.tensor_scalar(tmp, var, EPS_LN, 1.0, ALU.add, ALU.mult).then_inc(s, 1)
                pool.tensor_scalar(neg, mean, -1.0, 1.0, ALU.mult, ALU.mult).then_inc(s, 1)
                pool.wait_ge(s, k0 + 2)
                pool.tensor_tensor(rstd, tmp, nhalf[:, 0:n], ALU.pow).then_inc(s, 1)
                pool.wait_ge(s, k0 + 3)
                pool.tensor_tensor(shift, neg, rstd, ALU.mult).then_inc(s, 1)

            for b in range(B):
                t = slice(b * TB, (b + 1) * TB)
                pool.wait_ge(mv1_done, (b + 1) * TB)
                rstd_shift(mv1[:, t, 0], mv1[:, t, 1], ln1[:, 2, t], ln1[:, 0, t], ln1[:, 3, t],
                           ln1[:, 1, t], TB, ln1_done, 4 * b)
            def w_scale(u, slot, n):
                pool.wait_ge(whi_done, 2 * u + 2)
                held(1 + slot)
                rw, rd = raw_w(slot, n), raw_d(slot, n)
                pool.tensor_scalar(rw, rw, W_SCALE, 1.0, ALU.mult, ALU.mult).then_inc(wsc_done, 1)
                pool.tensor_scalar(rd, rd, W_SCALE, 1.0, ALU.mult, ALU.mult).then_inc(wsc_done, 1)

            def low_w(u, slot, dst_w, n):
                pool.wait_ge(wsc_done, 2 * u + 1)
                pool.tensor_tensor(dst_w[:, 1, :, :, 0:n], raw_w(slot, n), dst_w[:, 0, :, :, 0:n],
                                   ALU.subtract).then_inc(wlo_done, 1)

            def low_d(u, slot, dst_d, n):
                pool.wait_ge(wsc_done, 2 * u + 2)
                pool.tensor_tensor(dst_d[0:n, 1, :], raw_d(slot, n), dst_d[0:n, 0, :],
                                   ALU.subtract).then_inc(wlo_done, 1)

            def w_low(u, slot, dst_w, dst_d, n):
                w_scale(u, slot, n)
                low_w(u, slot, dst_w, n)
                low_d(u, slot, dst_d, n)

            def w_low_shared(m, slot):
                w_low(m, slot, sw[:, m], sd[:, m], P)

            w_scale(0, 0, P)
            pool.wait_ge(amax_done, 2)
            pool.partition_all_reduce(gmax[:], amax[:], P, bass.bass_isa.ReduceOp.max).then_inc(gmax_done, 1)
            w_scale(1, 1, P)

            pool.wait_ge(small_in, 64)
            pool.wait_ge(gmax_done, 5)
            held()
            pool.tensor_scalar(mask_res[:, 0, :], mask_raw[:], sc[:, 2:3], 1.0, ALU.mult, ALU.mult).then_inc(
                mask_done, 1)
            for i in range(3):
                pool.wait_ge(mask_done, 1 + 2 * i)
                pool.tensor_scalar(mask_b[:, i, :], mask_res[:, i, :], 1.0, 1.0, ALU.mult, ALU.mult).then_inc(
                    mask_done, 1)
                if i < 2:
                    pool.wait_ge(mask_done, 2 + 2 * i)
                    pool.tensor_tensor(mask_res[:, i + 1, :], mask_res[:, i, :], mask_b[:, i, :],
                                       ALU.subtract).then_inc(mask_done, 1)

            def round_ctx(c):
                seq = pool_seq(c)
                v, v20p = pv[:, seq % 2, 0, :], pv[:, seq % 2, 1, :]
                pool.wait_ge(pbits_done, 2 * seq + 2)
                pool.tensor_tensor(v, v20p, v, ALU.add).then_inc(pround, 1)
                pool.wait_ge(pround, seq + 1)
                pool.tensor_tensor(ctx_q[:, c, 0:D], v20p, v, ALU.subtract).then_inc(pq_done, 1)

            round_ctx(1)
            round_ctx(3)
            low_w(0, 0, sw[:, 0], P)
            low_d(0, 0, sd[:, 0], P)

            def ln_small(t, par):
                pool.wait_ge(mv2_done, t + 1)
                if not isinstance(t, int) or t >= 2:
                    pool.wait_ge(h_done, t - 1)
                rstd_shift(mv2[:, par, 0:1], mv2[:, par, 1:2], ln2[:, par, 2:3], ln2[:, par, 0:1],
                           ln2[:, par, 3:4], ln2[:, par, 1:2], 1, ln2_done, 4 * t)

            def w_low_expert(u, slot, par, c):
                w_low(u, slot, ew[:, par, c], ed[:, par, c], EC[c])

            for i in range(1, PS):
                ln_small(i - 1, (i - 1) % 2)
                for c in C_ROUND[i]:
                    round_ctx(c)
                if i == 4:
                    low_w(1, 1, sw[:, 1], P)
                if i == 5:
                    low_d(1, 1, sd[:, 1], P)
            with pool.Fori(0, 4) as r:
                for h in range(2):
                    ln_small(5 + 2 * r + h, (5 + h) % 2)
                    w_low_shared(2 + 2 * r + h, h)
            ln_small(13, 1)
            w_low_shared(MS - 1, 0)
            ln_small(14, 0)
            ln_small(15, 1)

            pool.wait_ge(table_zeroed, 16)
            pool.wait_ge(slots_done, 2)
            for t in range(NT):
                for k in range(TOPK):
                    i = TOPK * t + k
                    pool.indirect_dma_start(
                        out=slot_dram, out_offset=bass.IndirectOffsetOnAxis(ap=to_slot[:, i:i + 1], axis=0),
                        in_=tok_id[:, t:t + 1], in_offset=None, bounds_check=E * CAP - 1,
                        oob_is_err=False).then_inc(scattered, 16)
            for c in range(2):
                w_low_expert(MS + c, (MS + c) % 2, 0, c)

            def gather_expert(e):
                if e:
                    pool.wait_ge(xT_ps, CT * e)
                for j in range(CT):
                    pool.indirect_dma_start(
                        out=grow[:, j, :], out_offset=None, in_=h_dram,
                        in_offset=bass.IndirectOffsetOnAxis(ap=slot_tok[:, e, j:j + 1], axis=0),
                        bounds_check=T - 1, oob_is_err=False).then_inc(g_in, 16)

            pool.wait_ge(table_in, 16)
            gather_expert(0)
            w_low_expert(MS + 2, (MS + 2) % 2, 0, 2)
            for e in range(E):
                if e + 1 < E:
                    gather_expert(e + 1)
                    for c in range(ME):
                        u = MS + ME * (e + 1) + c
                        w_low_expert(u, u % 2, (e + 1) % 2, c)

            pool.wait_ge(o_stored, 16 * E)
            pool.wait_ge(xT_ps, CT * E)
            for q in range(NT):
                t = (q + NT // 2) % NT
                if q >= 2:
                    pool.wait_ge(c_done, q - 1)
                for k in range(TOPK):
                    i = TOPK * t + k
                    pool.indirect_dma_start(
                        out=comb[:, q % 2, k, :], out_offset=None, in_=eo_dram,
                        in_offset=bass.IndirectOffsetOnAxis(ap=from_slot[:, i:i + 1], axis=0),
                        bounds_check=E * CAP - 1, oob_is_err=False).then_inc(cg_in[q % 2], 16)

        @block.scalar
        def _(act):
            act.wait_ge(consts, 6)
            act.activation(carry_a[:], nhalf[:, 0:2], ACT.Silu)
            for t in range(NT):
                act.wait_ge(ln1_done, 4 * (t // TB + 1))
                if t >= 4:
                    act.wait_ge(zmax_done, t - 3)
                if t == NT // 2:
                    act.wait_ge(small_in, 64)
                    act.activation(tg[:], tg_raw[:], ACT.Tanh).then_inc(gates_done, 1)
                    act.mul(r_split[:, :, 0:E], r_raw[:], W_SCALE).then_inc(router_hi, 1)
                act.activation(gu4[:, t % 4, :], tok[:, t, :], ACT.Abs, bias=ln1[:, 1, t:t + 1],
                               scale=ln1[:, 0, t:t + 1]).then_inc(absz_done, 1)

            def quant(seq, par, alone, src, scale, bias):
                bank, depth = v_bank(seq, alone)
                if not isinstance(seq, int) or seq >= depth:
                    act.wait_ge(q_done, seq + 1 - depth)
                act.activation(bank, src, ACT.Identity, bias=bias, scale=scale).then_inc(v_done, 1)
                act.wait_ge(v_done, seq + 1)
                if depth > 1 and seq >= 2:
                    act.wait_ge(q_done, seq - 1)
                act.activation(v20[:, par, :], bank, ACT.Copy, scale=ROUND_UP).then_inc(v20_done, 1)

            def quant_ctx(c, seq, par, alone):
                quant(seq, par, alone, ctx_raw[:, c, :], sc[:, 1:2], 0.0)

            def quant_ctx_pool(c):
                seq = pool_seq(c)
                if seq >= 2:
                    act.wait_ge(pq_done, seq - 1)
                act.activation(pv[:, seq % 2, 0, :], ctx_raw[:, c, :], ACT.Identity, bias=0.0,
                               scale=sc[:, 1:2]).then_inc(pv_done, 1)

            def quant_x(t, seq, par, alone):
                quant(seq, par, alone, tok[:, t, :], vsc[:, 0, t:t + 1] if isinstance(t, int) else
                      vsc[:, 0, bass.ds(t, 1)], vsc[:, 1, t:t + 1] if isinstance(t, int) else
                      vsc[:, 1, bass.ds(t, 1)])

            def w_high(u, slot, half, dst_w, dst_d, n):
                act.wait_ge(raw_in[slot], 48 * (half + 1))
                act.mul(dst_w[:, 0, :, :, 0:n], raw_w(slot, n), W_SCALE).then_inc(whi_done, 1)
                act.mul(dst_d[0:n, 0, :], raw_d(slot, n), W_SCALE).then_inc(whi_done, 1)

            def silu(n, par, dst, rows, cols):
                act.wait_ge(gu_ps, n + 1)
                act.activation(sg[0:rows, par, 0:cols], gu[0:rows, par, 0, 0:cols], ACT.Silu,
                               scale=1.0 / (H_SCALE * W_SCALE)).then_inc(silu_done, 1)

            def act_high(n, par, dst, rows, cols):
                act.wait_ge(prod_done, n + 1)
                act.copy(dst, gu[0:rows, par, 0, 0:cols]).then_inc(ahi_done, 1)

            def chunk(*job):
                silu(*job)
                act_high(*job)

            def q_transposed(i, p):
                act.wait_ge(qT_ps, i + 1)
                if i >= 2:
                    act.wait_ge(xa_ps, i - 1)
                act.copy(qT[:, p], tp_q).then_inc(qT_done, 1)

            def step(i, p, half, alone, s, mlp=None, unit=None):
                if mlp:
                    silu(*mlp)
                if s["q"] and not alone:
                    quant_x(i + 1, seq_x(i), seq_x(i) % 2 if isinstance(i, int) else 1, alone)
                if unit:
                    w_high(*unit)
                if s["th"]:
                    act.wait_ge(x1_stored[p], 16 * half)
                    act.wait_ge(hT_ps, i - 1)
                    act.mul(h_split[:, i - 2, 0], tp_h, H_SCALE).then_inc(hhi_done, 1)
                if mlp:
                    act_high(*mlp)
                if s["tq"] and alone and i:
                    q_transposed(i, p)
                if alone:
                    for t in X_AHEAD[i]:
                        quant_x(t, seq_x(t - 1), t % 2, True)
                    for c in C_AHEAD[i]:
                        quant_ctx_pool(c)
                if s["ctx"] and not alone:
                    quant_ctx(i + 4, seq_ctx(i), 0, alone)
                if s["xa"]:
                    act.wait_ge(ln2_done, 4 * i)
                    if not isinstance(i, int) or i >= 3:
                        act.wait_ge(hT_ps, i - 2)
                        act.wait_ge(h_stored[1 - p], 16 * (half + p - 1))
                    act.activation(h_tok[:, 1 - p, :], tok[:, i - 1, :], ACT.Identity,
                                   bias=ln2[:, 1 - p, 1:2], scale=ln2[:, 1 - p, 0:1]).then_inc(h_done, 1)

            def job(m, par):
                return m, par, a_sh[:, m, 0, :], P, D

            def unit(m, slot, half):
                return m, slot, half, sw[:, m], sd[:, m], P

            w_high(*unit(0, 0, 0))
            w_high(*unit(1, 1, 0))
            act.wait_ge(scale_done, 1)
            quant_ctx_pool(1)
            quant_x(0, 0, 0, True)
            quant_ctx_pool(3)
            quant_ctx(0, 1, 1, True)
            q_transposed(0, 0)
            quant_ctx(2, 2, 0, True)
            for i in range(PS):
                step(i, i % 2, i // 2, True, stages(i))

            step(6, 0, 3, False, stages(6), job(0, 0), unit(2, 0, 1))
            with act.Fori(0, 2) as r:
                for h in range(2):
                    m = 2 * r + 1 + h
                    step(m + 6, 1 - h, r + (7 + h) // 2, False, stages(m), job(m, 1 - h),
                         unit(m + 2, 1 - h, r + (3 + h) // 2))
            for m in range(5, MS):
                i = m + 6
                step(i, i % 2, i // 2, False, stages(i), job(m, m % 2),
                     unit(m + 2, m % 2, (m + 2) // 2) if m + 2 < MS else None)
            step(NT + 1, 1, NT // 2, False, stages(NT + 1))
            act.wait_ge(gap_done, 1)
            act.activation(ex2[:], dlt[:], ACT.Exp, scale=1.0 / (H_SCALE * W_SCALE)).then_inc(exp_done, 1)
            act.activation(carry_a[:], tg_raw[:], ACT.Silu)
            def first_expert_unit(c):
                u = MS + c
                w_high(u, u % 2, u // 2, ew[:, 0, c], ed[:, 0, c], EC[c])

            act.wait_ge(xa_ps, NT)
            first_expert_unit(0)
            first_expert_unit(1)

            def block_chunks(b):
                n0 = block_job(b)
                with act.Fori(0, MS // 2) as r:
                    for h in range(2):
                        m = 2 * r + h
                        chunk(n0 + m, h, a_sh[:, m, 0, :], P, D)
                chunk(n0 + MS - 1, 0, a_sh[:, MS - 1, 0, :], P, D)

            block_chunks(1)
            first_expert_unit(2)

            def x_high(s, j, tpar):
                act.wait_ge(xT_ps, s + 1)
                act.mul(xe[:, 0, :, j * P:(j + 1) * P], tp_x[:, tpar], H_SCALE).then_inc(xhi_done, 1)

            def expert(e, h, r, last):
                for c in range(ME):
                    for half in range(2):
                        k = 2 * c + half
                        chunk(JOB_E + 2 * ME * e + k, k % 2, a_ex[0:EC[c], c, 0, half * HC:(half + 1) * HC],
                              EC[c], HC)
                    if not last:
                        u = MS + ME * (h + 1) + c
                        w_high(2 * ME * r + u, u % 2, ME * r + u // 2, ew[:, 1 - h, c], ed[:, 1 - h, c], EC[c])
                if not last:
                    x_high(CT * (e + 1), 0, (CT * (h + 1)) % 2)
                    x_high(CT * (e + 1) + 1, 1, (CT * (h + 1) + 1) % 2)
                if not isinstance(e, int) or e:
                    act.wait_ge(o_stored, 16 * e)
                for j in range(CT):
                    if not last and j >= 2:
                        x_high(CT * (e + 1) + j, j, (CT * (h + 1) + j) % 2)
                    act.wait_ge(o_ps, CT * e + j + 1)
                    act.mul(o_ex[:, j, :], dn[:, (CT * h + j) % 2, :], 1.0 / W_SCALE).then_inc(o_done, 1)

            for j in range(CT):
                x_high(j, j, j % 2)
            expert(0, 0, 0, False)
            with act.Fori(0, E // 2 - 1) as r:
                expert(2 * r + 1, 1, r, False)
                expert(2 * r + 2, 0, r + 1, False)
            expert(E - 1, 1, E // 2 - 1, True)
            n0 = block_job(2)
            for m in range(ME):
                chunk(n0 + m, m % 2, a_sh[:, m, 0, :], P, D)
            act.wait_ge(o_stored, 16 * E)
            with act.Fori(0, (MS - ME) // 2) as r:
                for h in range(2):
                    m = ME + 2 * r + h
                    chunk(n0 + m, 1 - h, a_sh[:, m, 0, :], P, D)
            block_chunks(3)

        @block.vector
        def _(dve):
            for t in range(NT):
                if t < 2 * TB:
                    dve.wait_ge(x_first[t], 16)
                elif t % TB == 0:
                    dve.wait_ge(x_in[t // TB - 2], 16)
                dve.bn_stats(st1[:, t, :], tok[:, t, :]).then_inc(bn1, 1)
                if t % TB == TB - 1:
                    for a in range(t - TB + 1, t + 1):
                        dve.wait_ge(bn1, a + 1)
                        dve.bn_aggr(mv1[:, a, :], st1[:, a, :]).then_inc(mv1_done, 1)
            for t in range(NT):
                dve.wait_ge(absz_done, t + 1)
                dve.tensor_reduce(zmax[:, t:t + 1], gu4[:, t % 4, :], AX.X, ALU.max).then_inc(zmax_done, 1)
                if t % TB == TB - 1:
                    b = t // TB
                    dve.wait_ge(c_in[b], 16)
                    dve.tensor_reduce(zmax[:, NT + b:NT + b + 1], ctx_raw[:, b * KD:(b + 1) * KD, :], AX.XY,
                                      ALU.max, apply_absolute_value=True).then_inc(cmax_done, 1)
            dve.wait_ge(gates_done, 1)
            dve.tensor_scalar(tgw[:], tg[:, 1:2], 1.0 / W_SCALE, None, ALU.mult).then_inc(tgw_done, 1)
            dve.wait_ge(router_hi, 1)
            dve.scalar_tensor_tensor(r_split[:, :, E:2 * E], r_raw[:], W_SCALE, r_split[:, :, 0:E],
                                     ALU.mult, ALU.subtract).then_inc(router_done, 1)
            dve.wait_ge(zmax_done, NT)
            dve.tensor_reduce(amax[:, 0:1], zmax[:, 0:NT], AX.X, ALU.max).then_inc(amax_done, 1)
            dve.wait_ge(cmax_done, B)
            dve.tensor_reduce(amax[:, 1:2], zmax[:, NT:NT + B], AX.X, ALU.max).then_inc(amax_done, 1)
            dve.wait_ge(gmax_done, 1)
            dve.tensor_scalar(sc[:, 4:6], gmax[:], EPS_Q, None, ALU.max).then_inc(gmax_done, 1)
            dve.wait_ge(gmax_done, 2)
            dve.reciprocal(sc[:, 6:8], sc[:, 4:6]).then_inc(gmax_done, 1)
            dve.wait_ge(gmax_done, 3)
            dve.tensor_scalar(sc[:, 0:2], sc[:, 6:8], FP8_MAX, None, ALU.mult).then_inc(gmax_done, 1)
            dve.wait_ge(gmax_done, 4)
            dve.wait_ge(ln1_done, 4 * B)
            dve.tensor_scalar(vsc[:, 0:2, :], ln1[:, 0:2, :], sc[:, 0:1], None, ALU.mult).then_inc(scale_done, 1)
            dve.tensor_scalar(sc[:, 2:3], sc[:, 0:1], sc[:, 1:2], None, ALU.mult).then_inc(gmax_done, 1)
            dve.wait_ge(gmax_done, 5)
            dve.reciprocal(sc[:, 4:5], sc[:, 2:3]).then_inc(gmax_done, 1)
            dve.wait_ge(gmax_done, 6)
            dve.tensor_scalar(sc[:, 3:4], sc[:, 4:5], tg[:, 0:1], None, ALU.mult).then_inc(gmax_done, 1)
            def held():
                dve.tensor_copy(carry_v[:], tgw[:])

            def quant(seq, par, alone, dst):
                q_bits(seq, par)
                q_round(seq, par, alone, dst)

            def q_bits(seq, par):
                u = v20[:, par, :].bitcast(U32)
                dve.wait_ge(v20_done, seq + 1)
                dve.tensor_scalar(u, u, EXP_MASK, HALF_BIT, ALU.bitwise_and, ALU.bitwise_or).then_inc(bits_done, 1)

            def q_round(seq, par, alone, dst):
                bank, _ = v_bank(seq, alone)
                dve.wait_ge(bits_done, seq + 1)
                dve.scalar_tensor_tensor(bank, v20[:, par, :], ROUND_FLOOR, bank, ALU.max,
                                         ALU.add).then_inc(sum_done, 1)
                dve.wait_ge(sum_done, seq + 1)
                dve.scalar_tensor_tensor(dst, v20[:, par, :], ROUND_FLOOR, bank, ALU.max,
                                         ALU.subtract).then_inc(q_done, 1)

            def quant_ctx(c, seq, par, alone):
                quant(seq, par, alone, ctx_q[:, c, 0:D])

            def bits_for_pool(c):
                seq = pool_seq(c)
                big = pv[:, seq % 2, 1, :]
                dve.wait_ge(pv_done, seq + 1)
                dve.tensor_scalar(big.bitcast(U32), pv[:, seq % 2, 0, :].bitcast(U32), EXP_MASK, HALF_BIT,
                                  ALU.bitwise_and, ALU.bitwise_or).then_inc(pbits_done, 1)
                dve.wait_ge(pbits_done, 2 * seq + 1)
                dve.tensor_scalar(big, big, ROUND_FLOOR / ROUND_UP, ROUND_UP, ALU.max,
                                  ALU.mult).then_inc(pbits_done, 1)

            def quant_x(t, tpar, seq, par, alone):
                if not isinstance(t, int) or t >= 2:
                    dve.wait_ge(qT_ps, t - 1)
                quant(seq, par, alone, q_tok[:, tpar, :])

            dve.wait_ge(gmax_done, 7)

            def prod(n, par, dst_hi, dst_lo, rows, cols):
                dve.wait_ge(silu_done, n + 1)
                dve.scalar_tensor_tensor(gu[0:rows, par, 0, 0:cols], gu[0:rows, par, 1, 0:cols],
                                         1.0 / (H_SCALE * W_SCALE), sg[0:rows, par, 0:cols], ALU.mult,
                                         ALU.mult).then_inc(prod_done, 1)

            def act_low(n, par, dst_hi, dst_lo, rows, cols):
                dve.wait_ge(ahi_done, n + 1)
                dve.tensor_tensor(dst_lo, gu[0:rows, par, 0, 0:cols], dst_hi, ALU.subtract).then_inc(alo_done, 1)

            def chunk(*job):
                prod(*job)
                act_low(*job)

            def job(n, m, par):
                return n, par, a_sh[:, m, 0, :], a_sh[:, m, 1, :], P, D

            def h_low(i):
                dve.wait_ge(hhi_done, i - 1)
                dve.scalar_tensor_tensor(h_split[:, i - 2, 1].rearrange("p k n -> p (k n)"), tp[:, 1, :],
                                         H_SCALE, h_split[:, i - 2, 0].rearrange("p k n -> p (k n)"),
                                         ALU.mult, ALU.subtract).then_inc(hlo_done, 1)

            def step(i, p, alone, s, mlp=None):
                if mlp:
                    prod(*mlp)
                if s["xa"]:
                    dve.wait_ge(xa_ps, i)
                    dve.scalar_tensor_tensor(tok[:, i - 1, :], dn[:, 0, :], sc[:, 3:4], tok[:, i - 1, :],
                                             ALU.mult, ALU.add).then_inc(x1_done, 1)
                    dve.wait_ge(x1_done, i)
                    held()
                    dve.bn_stats(st2[:, 1 - p, :], tok[:, i - 1, :]).then_inc(bn2, 1)
                    dve.wait_ge(bn2, i)
                    if not isinstance(i, int) or i >= 3:
                        dve.wait_ge(ln2_done, 4 * (i - 2))
                    held()
                    dve.bn_aggr(mv2[:, 1 - p, :], st2[:, 1 - p, :]).then_inc(mv2_done, 1)
                if s["q"] and not alone:
                    quant_x(i + 1, 1 - p, seq_x(i), seq_x(i) % 2 if isinstance(i, int) else 1, alone)
                if s["th"]:
                    h_low(i)
                if mlp:
                    act_low(*mlp)
                if s["tq"] and not alone:
                    dve.wait_ge(qT_ps, i + 1)
                    dve.wait_ge(xa_ps, i - 1)
                    dve.tensor_copy(qT[:, p], tp_q).then_inc(qT_done, 1)
                if s["ctx"] and alone:
                    for c in C_ROUND[i]:
                        bits_for_pool(c)
                elif s["ctx"]:
                    quant_ctx(i + 4, seq_ctx(i), 0, alone)
                if s["q"] and alone:
                    quant_x(i + 1, 1 - p, seq_x(i), seq_x(i) % 2, alone)

            def chunk_sh(n, m, par):
                chunk(*job(n, m, par))

            bits_for_pool(1)
            quant_x(0, 0, 0, 0, True)
            bits_for_pool(3)
            quant_ctx(0, 1, 1, True)
            quant_ctx(2, 2, 0, True)
            for i in range(PS):
                step(i, i % 2, True, stages(i))
            step(6, 0, False, stages(6), job(0, 0, 0))
            with dve.Fori(0, 2) as r:
                for h in range(2):
                    m = 2 * r + 1 + h
                    step(m + 6, 1 - h, False, stages(m), job(m, m, 1 - h))
            for m in range(5, MS):
                step(m + 6, m % 2, False, stages(m + 6), job(m, m, m % 2))
            step(NT + 1, 1, False, stages(NT + 1))

            def y_tile(b, j):
                y = b * TB + j
                dve.wait_ge(dn_ps, y + 1)
                dst = base[:, j if b < 3 else j + TB, :]
                if b < 2:
                    dve.wait_ge(base_in[j], 16 * (b + 1))
                dve.scalar_tensor_tensor(dst, dn[:, j % 2, :], tgw[:, 0:1], dst, ALU.mult,
                                         ALU.add).then_inc(y_done, 1)

            y_tile(0, 0)

            k = [0]

            def link(ins):
                k[0] += 1
                ins.then_inc(rstep, 1)
                dve.wait_ge(rstep, k[0])

            dve.wait_ge(rt_ps, NT)
            link(dve.tensor_reduce(lg[:], tp_r.rearrange("p t (s e) -> p t e s", s=2), AX.X, ALU.add))
            for t in range(NT):
                ins = dve.max(top_v[:, t, :], lg[:, t, :])
                ins.then_inc(rstep, 1)
                k[0] += 1
            dve.wait_ge(rstep, k[0])
            for t in range(NT):
                ins = dve.max_index(top_i[:, t, :], top_v[:, t, :], lg[:, t, :])
                ins.then_inc(rstep, 1)
                k[0] += 1
            dve.wait_ge(rstep, k[0])
            dve.tensor_tensor(dlt[:], top_v[:, :, 1], top_v[:, :, 0], ALU.subtract).then_inc(gap_done, 1)
            link(dve.tensor_copy(sel[:], top_i[:, :, 0:TOPK]))
            dve.wait_ge(consts, 12)
            link(dve.tensor_tensor(
                hot[:].rearrange("p t k e -> p (t k) e"),
                sel[:].rearrange("p t k -> p (t k)").unsqueeze(2).to_broadcast([P, NT * TOPK, E]),
                iota_e[:].unsqueeze(1).to_broadcast([P, NT * TOPK, E]), ALU.is_equal))
            dve.tensor_tensor(hot_n[:], hot[:, :, 0, :], hot[:, :, 1, :], ALU.add).then_inc(cnt_ready, 1)
            y_tile(0, 1)
            dve.wait_ge(pos_ps, 1)
            for kk in range(TOPK):
                ins = dve.tensor_tensor(seat[:, :, kk, :], hot[:, :, kk, :],
                                        tp_pos.rearrange("p (t e) -> p t e", t=NT), ALU.mult)
                ins.then_inc(rstep, 1)
                k[0] += 1
            dve.wait_ge(rstep, k[0])
            link(dve.tensor_reduce(pos[:], seat[:].rearrange("p t k e -> p (t k) e"), AX.X, ALU.add))
            link(dve.tensor_scalar(valid[:], pos[:], float(CAP), None, ALU.is_lt))
            link(dve.tensor_scalar(slot_f[:], pos[:], float(CAP - 1), None, ALU.min))
            link(dve.scalar_tensor_tensor(pos[:], sel[:].rearrange("p t k -> p (t k)"), float(CAP), slot_f[:],
                                          ALU.mult, ALU.add))
            dve.tensor_copy(from_slot[:], pos[:]).then_inc(slots_done, 1)
            link(dve.tensor_scalar(slot_f[:], valid[:], -FAR, FAR, ALU.mult, ALU.add))
            dve.tensor_tensor(to_slot[:], pos[:], slot_f[:], ALU.add).then_inc(slots_done, 1)
            dve.wait_ge(exp_done, 1)
            link(dve.tensor_scalar(wsum[:], ex2[:], 1.0, None, ALU.add))
            link(dve.reciprocal(dlt[:], wsum[:]))
            link(dve.tensor_scalar(dlt[:], dlt[:], tg[:, 1:2], None, ALU.mult))
            vv = valid[:].rearrange("p (t k) -> p t k", k=TOPK)
            link(dve.tensor_tensor(wsum[:], dlt[:], ex2[:], ALU.mult))
            dve.tensor_tensor(cw[:, :, 0], dlt[:], vv[:, :, 0], ALU.mult).then_inc(weights_done, 1)
            dve.tensor_tensor(cw[:, :, 1], wsum[:], vv[:, :, 1], ALU.mult).then_inc(weights_done, 1)

            for j in range(2, TB):
                y_tile(0, j)

            n0 = block_job(1)
            with dve.Fori(0, MS // 2) as r:
                for h in range(2):
                    chunk_sh(n0 + 2 * r + h, 2 * r + h, h)
            chunk_sh(n0 + MS - 1, MS - 1, 0)
            def x_low(s, j, tpar):
                dve.wait_ge(xhi_done, s + 1)
                dve.scalar_tensor_tensor(xe[:, 1, :, j * P:(j + 1) * P], tp_x[:, tpar], H_SCALE,
                                         xe[:, 0, :, j * P:(j + 1) * P], ALU.mult,
                                         ALU.subtract).then_inc(xlo_done, 1)

            def expert(e, h, last):
                for c in range(ME):
                    for half in range(2):
                        kk = 2 * c + half
                        cols = slice(half * HC, (half + 1) * HC)
                        chunk(JOB_E + 2 * ME * e + kk, kk % 2, a_ex[0:EC[c], c, 0, cols],
                              a_ex[0:EC[c], c, 1, cols], EC[c], HC)
                if not last:
                    for j in range(CT):
                        x_low(CT * (e + 1) + j, j, (CT * (h + 1) + j) % 2)

            x_low(0, 0, 0)
            for j in range(TB):
                x_low(j + 1, j + 1, (j + 1) % 2)
                y_tile(1, j)
            expert(0, 0, False)
            with dve.Fori(0, E // 2 - 1) as r:
                expert(2 * r + 1, 1, False)
                expert(2 * r + 2, 0, False)
            expert(E - 1, 1, True)

            dve.wait_ge(weights_done, 2)

            def combine(q, t, p, half, place, ring):
                if ring:
                    dve.wait_ge(cring_in[p], 16 * (half - 3))
                else:
                    dve.wait_ge(cbase_in, 16 * NT // 2)
                dve.wait_ge(cg_in[p], 32 * (half + 1))
                dst = base[:, place, :]
                w = cw[:].rearrange("p t k -> p (t k)")
                dve.scalar_tensor_tensor(dst, comb[:, p, 0, :], w[:, bass.ds(TOPK * t, 1)], dst, ALU.mult,
                                         ALU.add).then_inc(c1_done, 1)
                dve.wait_ge(c1_done, q + 1)
                dve.scalar_tensor_tensor(dst, comb[:, p, 1, :], w[:, bass.ds(TOPK * t + 1, 1)], dst, ALU.mult,
                                         ALU.add).then_inc(c_done, 1)

            n0 = block_job(2)
            for m in range(2):
                chunk_sh(n0 + m, m, m)
            with dve.Fori(0, 4) as r:
                for h in range(2):
                    q = 2 * r + h
                    chunk_sh(n0 + q + 2, q + 2, h)
                    combine(q, q + 8, h, r, q, False)
            chunk_sh(n0 + MS - 1, MS - 1, 0)
            combine(8, 0, 0, 4, 8, True)
            for j in range(TB):
                y_tile(2, j)
            n0 = block_job(3)
            for m in range(7):
                q = 9 + m
                chunk_sh(n0 + m, m, m % 2)
                combine(q, q - 8, q % 2, q // 2, 8 + q % 2, True)
            for m in range(7, MS):
                chunk_sh(n0 + m, m, m % 2)
            for j in range(TB):
                y_tile(3, j)

        @block.tensor
        def _(pe):
            pe.wait_ge(consts, 12)

            def transpose_q(i, p):
                pe.wait_ge(q_done, x_ready(i))
                if not isinstance(i, int) or i >= 1:
                    pe.wait_ge(qT_done, i)
                for k in range(KD):
                    ins = pe.transpose(tp_q[:, k, :], q_tok[:, p, k * P:(k + 1) * P], id_b[:])
                ins.then_inc(qT_ps, 1)

            def step(i, p, s):
                if s["xa"]:
                    pe.wait_ge(qT_done, i)
                    if isinstance(i, int) and i < PS + 2:
                        if i in (5, 7):
                            pe.wait_ge(pq_done, i + 1)
                    else:
                        pe.wait_ge(q_done, seq_ctx(min(i - 2, LAST_CTX_STEP) if isinstance(i, int) else i - 2) + 1)
                    if not isinstance(i, int) or i >= 2:
                        pe.wait_ge(x1_done, i - 1)
                    b = (i - 1) // TB
                    first = isinstance(i, int) and i == 1
                    for k in (1, 0, 3, 2) if first else range(KD):
                        if first:
                            if k % 2:
                                pe.wait_ge(pq_done, pool_seq(k) + 1)
                            else:
                                pe.wait_ge(q_done, 2 + k // 2)
                        pe.matmul(dn[:, 0, :], qT[:, 1 - p, k, :], ctx_q[:, TB * b + k, 0:D],
                                  start=k == (1 if first else 0), stop=False)
                    if first:
                        pe.wait_ge(mask_in, 16)
                    pe.matmul(dn[:, 0, :], pick[:, b, :], mask_p[:], start=False, stop=True).then_inc(xa_ps, 1)
                if s["th"]:
                    pe.wait_ge(h_done, i - 1)
                    if not isinstance(i, int) or i >= 3:
                        pe.wait_ge(hlo_done, i - 2)
                    for k in range(KD):
                        ins = pe.transpose(tp_h[:, k, :], h_tok[:, p, k * P:(k + 1) * P], id_f[:])
                    ins.then_inc(hT_ps, 1)
                if s["rt"]:
                    pe.wait_ge(hlo_done, i - 2)
                    pe.wait_ge(qT_done, min(i, NT) if isinstance(i, int) else i)
                    if isinstance(i, int) and i == 3:
                        pe.wait_ge(router_done, 1)
                    for k in range(KD):
                        for part in range(2):
                            ins = pe.matmul(tp_r[:, i - 3, :], h_split[:, i - 3, part, k, :], r_split[:, k, :],
                                            start=k + part == 0, stop=k + part == KD)
                    ins.then_inc(rt_ps, 1)
                if s["tq"]:
                    transpose_q(i, p)

            def chunk_sh(n, b, m, par, free):
                if free is not None:
                    pe.wait_ge(alo_done, free)
                for g in range(2):
                    for k in range(KD):
                        for w, a in PARTS:
                            ins = pe.matmul(gu[:, par, g, :], sw[:, m, w, k, g, :],
                                            h_split[:, b * TB:(b + 1) * TB, a, k, :],
                                            start=k + w + a == 0, stop=k == KD - 1 and w == 1)
                ins.then_inc(gu_ps, 1)

            def down_sh(n0, y, j, par, wait):
                if wait:
                    pe.wait_ge(y_done, y - 1)
                for m in range(MS):
                    if m == 0:
                        pe.wait_ge(alo_done, n0 + MS - 1)
                    if m == MS - 1:
                        pe.wait_ge(alo_done, n0 + MS)
                    for w, a in PARTS:
                        ins = pe.matmul(dn[:, par, :], a_sh[:, m, a, bass.ds(j * P, P)], sd[:, m, w, :],
                                        start=m + w + a == 0, stop=m == MS - 1 and w == 1)
                ins.then_inc(dn_ps, 1)

            def block_chunks(b):
                n0 = block_job(b)
                chunk_sh(n0, b, 0, 0, n0)
                chunk_sh(n0 + 1, b, 1, 1, n0)
                with pe.Fori(1, MS // 2) as r:
                    for h in range(2):
                        m = 2 * r + h
                        chunk_sh(n0 + m, b, m, h, n0 + m - 1)
                chunk_sh(n0 + MS - 1, b, MS - 1, 0, n0 + MS - 2)

            def block_down(b):
                with pe.Fori(0, TB // 2) as r:
                    for h in range(2):
                        j = 2 * r + h
                        down_sh(block_job(b), b * TB + j, j, h, True)

            for i in range(FIRST_CHUNK_STEP + 1):
                step(i, i % 2, stages(i))
            pe.wait_ge(hlo_done, TB)
            pe.wait_ge(q_done, seq_x(FIRST_CHUNK_STEP - 2) + 1)

            def chunk_0(m, par, free):
                pe.wait_ge(wlo_done, 2 * m + 1)
                chunk_sh(m, 0, m, par, free)

            chunk_0(0, 0, None)
            step(6, 0, stages(6))
            pe.wait_ge(q_done, seq_x(PS - 1) + 1)
            chunk_0(1, 1, None)
            step(7, 1, stages(7))
            chunk_0(2, 0, 1)
            with pe.Fori(0, 2) as r:
                for h in range(2):
                    m = 3 + 2 * r + h
                    step(m + 5, h, stages(m))
                    chunk_0(m, 1 - h, m - 1)
            for m in range(7, MS):
                step(m + 5, (m + 5) % 2, stages(m + 5))
                chunk_0(m, m % 2, m - 1)
            step(NT, 0, stages(NT))
            pe.wait_ge(x1_done, NT)
            pe.wait_ge(q_done, x_ready(NT - 1))
            pe.wait_ge(wlo_done, 2 * MS)
            down_sh(0, 0, 0, 0, False)
            step(NT + 1, 1, stages(NT + 1))
            down_sh(0, 1, 1, 1, False)
            step(NT + 2, 0, stages(NT + 2))
            down_sh(0, 2, 2, 0, True)

            pe.wait_ge(cnt_ready, 1)
            pe.wait_ge(hlo_done, NT)
            counts = hot_n[:].rearrange("p t e -> p (t e)")
            pe.matmul(tp_pos, before[:], counts, start=True, stop=False)
            for t in range(1, NT):
                ins = pe.matmul(tp_pos[:, t * E:NT * E], ones_b[:], counts[:, 0:(NT - t) * E], start=False,
                                stop=t == NT - 1)
            ins.then_inc(pos_ps, 1)
            down_sh(0, 3, 3, 1, True)

            block_chunks(1)

            def transposes(s, j, par):
                if not isinstance(s, int) or s >= 2:
                    pe.wait_ge(xlo_done, s - 1)
                for k in range(KD):
                    ins = pe.transpose(tp_x[:, par, k, :], grow[:, j, k * P:(k + 1) * P], id_f[:])
                ins.then_inc(xT_ps, 1)

            pe.wait_ge(g_in, 16 * CT)
            transposes(0, 0, 0)
            for j in range(TB):
                transposes(j + 1, j + 1, (j + 1) % 2)
                down_sh(block_job(1), TB + j, j, j % 2, True)

            def expert(e, h, last):
                n0 = JOB_E + 2 * ME * e
                pe.wait_ge(xlo_done, CT * (e + 1))
                for c in range(ME):
                    pe.wait_ge(wlo_done, 2 * (MS + ME * e + c) + 1)
                    for half in range(2):
                        k6 = 2 * c + half
                        pe.wait_ge(alo_done, n0 + k6 - 1 if not (isinstance(e, int) and e == 0 and k6 < 2) else JOB_E)
                        for g in range(2):
                            for k in range(KD):
                                for w, a in PARTS:
                                    ins = pe.matmul(gu[0:EC[c], k6 % 2, g, 0:HC], ew[:, h, c, w, k, g, 0:EC[c]],
                                                    xe[:, a, k, half * HC:(half + 1) * HC],
                                                    start=k + w + a == 0, stop=k == KD - 1 and w == 1)
                        ins.then_inc(gu_ps, 1)
                if not last:
                    pe.wait_ge(g_in, 16 * CT * (e + 2))
                    transposes(CT * (e + 1), 0, (CT * (1 - h)) % 2)
                    transposes(CT * (e + 1) + 1, 1, (CT * (1 - h) + 1) % 2)
                def down(j, chunks):
                    for c in chunks:
                        for w, a in PARTS:
                            ins = pe.matmul(dn[:, (CT * h + j) % 2, :], a_ex[0:EC[c], c, a, j * P:(j + 1) * P],
                                            ed[0:EC[c], h, c, w, :], start=c + w + a == 0,
                                            stop=c == ME - 1 and w == 1)
                    return ins

                if isinstance(e, int) and e == 0:
                    pe.wait_ge(y_done, 2 * TB)
                else:
                    pe.wait_ge(o_done, CT * e)
                pe.wait_ge(wlo_done, 2 * (MS + ME * (e + 1)))
                pe.wait_ge(alo_done, n0 + 2 * ME - 2)
                for j in range(2):
                    down(j, range(ME - 1))
                pe.wait_ge(alo_done, n0 + 2 * ME)
                for j in range(2):
                    down(j, [ME - 1]).then_inc(o_ps, 1)
                for j in range(2, CT):
                    if not last:
                        transposes(CT * (e + 1) + j, j, (CT * (1 - h) + j) % 2)
                    pe.wait_ge(o_done, CT * e + j - 1)
                    down(j, range(ME)).then_inc(o_ps, 1)

            expert(0, 0, False)
            with pe.Fori(0, E // 2 - 1) as r:
                expert(2 * r + 1, 1, False)
                expert(2 * r + 2, 0, False)
            expert(E - 1, 1, True)

            for b in (2, 3):
                block_chunks(b)
                if b == 2:
                    pe.wait_ge(o_done, CT * E)
                block_down(b)


_INS = ["x", "ctx_2048", "mask_Bx1xS2_ff0", "g_xattn", "g_ffn", "L0_ffn_router", "L0_ffn_w_up_gate",
        "L0_ffn_w_down", "L0_ffn_shared_w_up_gate", "L0_ffn_shared_w_down"]


def kernel(**inputs):
    import numpy as np
    import concourse.bacc as bacc
    from concourse.bass_utils import run_bass_kernel_spmd

    nc = bacc.Bacc("TRN2", target_bir_lowering=False, num_devices=1)
    arrays, args = {}, []
    for name in _INS:
        a = np.ascontiguousarray(inputs[name])
        arrays[f"in_{name}"] = a
        args.append(nc.dram_tensor(f"in_{name}", a.shape, mybir.dt.from_np(a.dtype), kind="ExternalInput").ap())
    shape = arrays["in_x"].shape
    args.append(nc.dram_tensor("out_0", shape, F32, kind="ExternalOutput").ap())
    build_flamingo(nc, *args)
    r = run_bass_kernel_spmd(nc, [arrays], core_ids=[0])
    return r.results[0]["out_0"]
```
